# Optimizing a Trainium2 kernel written in Bass

```python
import numpy as np
import jax
import jax.numpy as jnp

def _softmax(x, axis=-1):
    return jax.nn.softmax(x, axis=axis)

def _gelu(x):
    return jax.nn.gelu(x, approximate=True)

def _silu(x):
    return jax.nn.silu(x)

def _sigmoid(x):
    return jax.nn.sigmoid(x)

def _layernorm(x, axis=-1, eps=1e-05):
    m = jnp.mean(x, axis=axis, keepdims=True)
    v = jnp.var(x, axis=axis, keepdims=True)
    return (x - m) / jnp.sqrt(v + eps)

def _scatter_add(tgt, idx, src, axis=0):
    return tgt.at[idx].add(src)

def _segment_sum(src, seg, n):
    return jax.ops.segment_sum(src, seg, n)
kernel_name = 'mk_adaln_d1_jaxref_r4_04c994'

def setup_inputs(seed: int=0):
    np.random.seed(seed)
    _w = jnp.asarray

    def _L0_attn_setup():
        import jax, jax.numpy as jnp
        import numpy as np
        B, T, HIDDEN = (2, 1024, 512)
        NUM_HEADS, HEAD_K, HEAD_V = (6, 64, 128)
        KEY_DIM, VALUE_DIM = (NUM_HEADS * HEAD_K, NUM_HEADS * HEAD_V)
        CONV_K, CHUNK, EPS = (4, 64, 1e-05)

        def short_conv(x, w):
            K = w.shape[1]
            xp = jnp.pad(x, ((0, 0), (K - 1, 0), (0, 0)))
            y = sum((xp[:, i:i + x.shape[1], :] * w[:, i] for i in range(K)))
            return jax.nn.silu(y)

        def l2norm(x):
            return x * jax.lax.rsqrt(jnp.sum(x * x, -1, keepdims=True))

        def _step(S, xs):
            qt, kt, vt, gt, bt = xs
            S = S * jnp.exp(gt)[..., None, None]
            pred = jnp.einsum('bhk,bhkv->bhv', kt, S)
            delta = (vt - pred) * bt[..., None]
            S = S + jnp.einsum('bhk,bhv->bhkv', kt, delta)
            return (S, jnp.einsum('bhk,bhkv->bhv', qt, S))

        def _chunk(S, xs):
            return jax.lax.scan(_step, S, xs)
        _chunk_ckpt = jax.checkpoint(_chunk)

        def gated_delta_rule(q, k, v, g, beta):
            b, t, h, dk = q.shape
            dv = v.shape[-1]
            q = l2norm(q) * dk ** (-0.5)
            k = l2norm(k)
            nc = t // CHUNK

            def to_scan(x):
                x = x.reshape(b, nc, CHUNK, *x.shape[2:])
                return jnp.moveaxis(x, 0, 2)
            xs = tuple(map(to_scan, (q, k, v, g, beta)))
            S0 = jnp.zeros((b, h, dk, dv), q.dtype)
            _, o = jax.lax.scan(_chunk_ckpt, S0, xs)
            return jnp.moveaxis(o, 2, 0).reshape(b, t, h, dv)
        key = jax.random.key(seed)
        ks = jax.random.split(key, 14)

        def lin(k, fi, fo):
            return jax.random.normal(k, (fi, fo), jnp.float32) / np.sqrt(fi)
        A = jax.random.uniform(ks[11], (NUM_HEADS,), minval=0.001, maxval=16.0)
        dt = jnp.exp(jax.random.uniform(ks[12], (NUM_HEADS,)) * (np.log(0.1) - np.log(0.001)) + np.log(0.001))
        dt = jnp.clip(dt, 0.0001)
        return {'hidden_states': jax.random.normal(ks[0], (B, T, HIDDEN), jnp.float32), 'Wq': lin(ks[1], HIDDEN, KEY_DIM), 'Wk': lin(ks[2], HIDDEN, KEY_DIM), 'Wv': lin(ks[3], HIDDEN, VALUE_DIM), 'Wa': lin(ks[4], HIDDEN, NUM_HEADS), 'Wb': lin(ks[5], HIDDEN, NUM_HEADS), 'Wg': lin(ks[6], HIDDEN, VALUE_DIM), 'Wo': lin(ks[7], VALUE_DIM, HIDDEN), 'conv_wq': jax.random.normal(ks[8], (KEY_DIM, CONV_K), jnp.float32) / np.sqrt(CONV_K), 'conv_wk': jax.random.normal(ks[9], (KEY_DIM, CONV_K), jnp.float32) / np.sqrt(CONV_K), 'conv_wv': jax.random.normal(ks[10], (VALUE_DIM, CONV_K), jnp.float32) / np.sqrt(CONV_K), 'A_log': jnp.log(A), 'dt_bias': dt + jnp.log(-jnp.expm1(-dt)), 'norm_weight': jnp.ones((HEAD_V,), jnp.float32)}
    _L0_attn_in = _L0_attn_setup()

    def _L0_ffn_setup():
        import jax, jax.numpy as jnp
        import numpy as np
        DIM_IN = 512
        DIM_HIDDEN = 2048
        key = jax.random.key(seed)
        k_x, k_g, k_u, k_d = jax.random.split(key, 4)
        s_in = 1.0 / np.sqrt(DIM_IN)
        s_hid = 1.0 / np.sqrt(DIM_HIDDEN)
        x = jax.random.normal(k_x, (4, 512, DIM_IN), dtype=jnp.float32)
        w_gate = jax.random.uniform(k_g, (DIM_HIDDEN, DIM_IN), jnp.float32, -s_in, s_in)
        w_up = jax.random.uniform(k_u, (DIM_HIDDEN, DIM_IN), jnp.float32, -s_in, s_in)
        w_down = jax.random.uniform(k_d, (DIM_IN, DIM_HIDDEN), jnp.float32, -s_hid, s_hid)
        return {'x': x, 'w_gate': w_gate, 'w_up': w_up, 'w_down': w_down}
    _L0_ffn_in = _L0_ffn_setup()
    _L0_c = _w((lambda *s: np.random.randn(*s).astype(np.float32) * 0.05)(4, 512))
    _L0_wmod = _w((lambda *s: np.random.randn(*s).astype(np.float32) * 0.05)(512, 6 * 512) * 512 ** (-0.5))
    _d = {'L0_attn_hidden_states': _L0_attn_in['hidden_states'], 'L0_attn_Wq': _L0_attn_in['Wq'], 'L0_attn_Wk': _L0_attn_in['Wk'], 'L0_attn_Wv': _L0_attn_in['Wv'], 'L0_attn_Wa': _L0_attn_in['Wa'], 'L0_attn_Wb': _L0_attn_in['Wb'], 'L0_attn_Wg': _L0_attn_in['Wg'], 'L0_attn_Wo': _L0_attn_in['Wo'], 'L0_attn_conv_wq': _L0_attn_in['conv_wq'], 'L0_attn_conv_wk': _L0_attn_in['conv_wk'], 'L0_attn_conv_wv': _L0_attn_in['conv_wv'], 'L0_attn_A_log': _L0_attn_in['A_log'], 'L0_attn_dt_bias': _L0_attn_in['dt_bias'], 'L0_attn_norm_weight': _L0_attn_in['norm_weight'], 'L0_ffn_w_gate': _L0_ffn_in['w_gate'], 'L0_ffn_w_up': _L0_ffn_in['w_up'], 'L0_ffn_w_down': _L0_ffn_in['w_down'], 'L0_c': _L0_c, 'L0_wmod': _L0_wmod}
    _x0 = _d['L0_attn_hidden_states']
    _d['L0_attn_hidden_states'] = jax.random.normal(jax.random.fold_in(jax.random.key(seed), 1), (4, 512, 512), dtype=_x0.dtype)
    del _x0
    return _d

def reference(L0_attn_hidden_states, L0_attn_Wq, L0_attn_Wk, L0_attn_Wv, L0_attn_Wa, L0_attn_Wb, L0_attn_Wg, L0_attn_Wo, L0_attn_conv_wq, L0_attn_conv_wk, L0_attn_conv_wv, L0_attn_A_log, L0_attn_dt_bias, L0_attn_norm_weight, L0_ffn_w_gate, L0_ffn_w_up, L0_ffn_w_down, L0_c, L0_wmod):

    def _L0_attn_ref(hidden_states, Wq, Wk, Wv, Wa, Wb, Wg, Wo, conv_wq, conv_wk, conv_wv, A_log, dt_bias, norm_weight):
        import jax, jax.numpy as jnp
        import numpy as np
        B, T, HIDDEN = (2, 1024, 512)
        NUM_HEADS, HEAD_K, HEAD_V = (6, 64, 128)
        KEY_DIM, VALUE_DIM = (NUM_HEADS * HEAD_K, NUM_HEADS * HEAD_V)
        CONV_K, CHUNK, EPS = (4, 64, 1e-05)

        def short_conv(x, w):
            K = w.shape[1]
            xp = jnp.pad(x, ((0, 0), (K - 1, 0), (0, 0)))
            y = sum((xp[:, i:i + x.shape[1], :] * w[:, i] for i in range(K)))
            return jax.nn.silu(y)

        def l2norm(x):
            return x * jax.lax.rsqrt(jnp.sum(x * x, -1, keepdims=True))

        def _step(S, xs):
            qt, kt, vt, gt, bt = xs
            S = S * jnp.exp(gt)[..., None, None]
            pred = jnp.einsum('bhk,bhkv->bhv', kt, S)
            delta = (vt - pred) * bt[..., None]
            S = S + jnp.einsum('bhk,bhv->bhkv', kt, delta)
            return (S, jnp.einsum('bhk,bhkv->bhv', qt, S))

        def _chunk(S, xs):
            return jax.lax.scan(_step, S, xs)
        _chunk_ckpt = jax.checkpoint(_chunk)

        def gated_delta_rule(q, k, v, g, beta):
            b, t, h, dk = q.shape
            dv = v.shape[-1]
            q = l2norm(q) * dk ** (-0.5)
            k = l2norm(k)
            nc = t // CHUNK

            def to_scan(x):
                x = x.reshape(b, nc, CHUNK, *x.shape[2:])
                return jnp.moveaxis(x, 0, 2)
            xs = tuple(map(to_scan, (q, k, v, g, beta)))
            S0 = jnp.zeros((b, h, dk, dv), q.dtype)
            _, o = jax.lax.scan(_chunk_ckpt, S0, xs)
            return jnp.moveaxis(o, 2, 0).reshape(b, t, h, dv)
        b, t, _ = hidden_states.shape
        q = short_conv(hidden_states @ Wq, conv_wq).reshape(b, t, NUM_HEADS, HEAD_K)
        k = short_conv(hidden_states @ Wk, conv_wk).reshape(b, t, NUM_HEADS, HEAD_K)
        v = short_conv(hidden_states @ Wv, conv_wv).reshape(b, t, NUM_HEADS, HEAD_V)
        beta = jax.nn.sigmoid(hidden_states @ Wb)
        g = -jnp.exp(A_log) * jax.nn.softplus(hidden_states @ Wa + dt_bias)
        o = gated_delta_rule(q, k, v, g, beta)
        gate = (hidden_states @ Wg).reshape(b, t, NUM_HEADS, HEAD_V)
        o = o * jax.lax.rsqrt(jnp.mean(o * o, -1, keepdims=True) + EPS) * norm_weight
        o = o * jax.nn.silu(gate)
        return o.reshape(b, t, VALUE_DIM) @ Wo

    def _L0_ffn_ref(x, w_gate, w_up, w_down):
        import jax, jax.numpy as jnp
        import numpy as np
        DIM_IN = 512
        DIM_HIDDEN = 2048
        gate = jnp.einsum('bsd,hd->bsh', x, w_gate)
        up = jnp.einsum('bsd,hd->bsh', x, w_up)
        gated = jax.nn.silu(gate) * up
        return jnp.einsum('bsh,dh->bsd', gated, w_down)
    x = L0_attn_hidden_states
    mod = (_silu(L0_c) @ L0_wmod).reshape(L0_c.shape[0], 6, 1, -1)
    sa, ca, ga, sb, cb, gb = (mod[:, 0], mod[:, 1], mod[:, 2], mod[:, 3], mod[:, 4], mod[:, 5])
    ga = (2 * (ga >= 0) - 1) * jnp.maximum(jnp.abs(ga), 0.25)
    gb = (2 * (gb >= 0) - 1) * jnp.maximum(jnp.abs(gb), 0.25)
    h = _layernorm(x, axis=-1) * (1 + ca) + sa
    x = x + ga * _L0_attn_ref(h, L0_attn_Wq, L0_attn_Wk, L0_attn_Wv, L0_attn_Wa, L0_attn_Wb, L0_attn_Wg, L0_attn_Wo, L0_attn_conv_wq, L0_attn_conv_wk, L0_attn_conv_wv, L0_attn_A_log, L0_attn_dt_bias, L0_attn_norm_weight)
    h = _layernorm(x, axis=-1) * (1 + cb) + sb
    x = x + gb * _L0_ffn_ref(h, L0_ffn_w_gate, L0_ffn_w_up, L0_ffn_w_down)
    return x

_drawn_inputs = setup_inputs


def setup_inputs(seed=0):
    import zlib

    import numpy as np

    out = dict(_drawn_inputs(seed))
    spreads = {'L0_attn_norm_weight': (1.0, 0.6)}
    factors = {'L0_attn_A_log': 3.091, 'L0_attn_Wa': 2.741}
    for name, (base, spread) in spreads.items():
        noise = np.random.default_rng([zlib.crc32(name.encode()), seed]).standard_normal(out[name].shape)
        drawn = base * np.exp(spread * noise) if base else spread * noise
        out[name] = jnp.asarray(drawn.astype(out[name].dtype))
    for name, factor in factors.items():
        out[name] = (out[name] * factor).astype(out[name].dtype)
    return out
```

```python
import numpy as np
import concourse.bass as bass
from concourse import mybir

NB, SEQ, D, H, DK, DV, FF = 4, 512, 512, 6, 64, 128, 2048
NS = SEQ // 128
HEADS = [0, 2, 4, 1, 3, 5]
EPS = 1e-5
NT1 = 19
CONSTS = ["ident", "SG", "LE", "CH0", "CH1", "BO", "ON", "EP", "LL"]


def constants():
    i = np.arange(128)
    r, c = i[:, None], i[None, :]
    same = (r // 64) == (c // 64)
    m = {
        "ident": r == c,
        "SG": (r > c) & same,
        "LE": (r <= c) & same,
        "CH0": (r < 64) & (c >= 0),
        "CH1": (r >= 64) & (c >= 0),
        "BO": same,
        "ON": np.full((128, 128), 1.0 / 128),
        "EP": np.full((128, 128), EPS * DK),
        "LL": same & (r % 64 >= 32) & (c % 64 < 32),
    }
    cols = [m[n].astype(np.float32) for n in CONSTS]
    sel = np.zeros((128, NB * 128), np.float32)
    for b in range(NB):
        sel[b, b * 128:(b + 1) * 128] = 1.0
    extra = np.zeros((128, 8), np.float32)
    extra[:, 0] = EPS
    extra[:, 1] = 1.0
    return np.ascontiguousarray(np.concatenate(cols + [sel, extra], axis=1))


class Eng:

    def __init__(self, sem):
        self.sem, self.n, self.q, self.seen = sem, 0, [], {}

    def wait(self, *toks):
        for t in toks:
            if t is None:
                continue
            if isinstance(t, (list, tuple)) and t and isinstance(t[0], (list, tuple)):
                self.wait(*t)
                continue
            if not t:
                continue
            sem, v = t
            if self.seen.get(id(sem), 0) < v:
                self.seen[id(sem)] = v
                self.q.append(lambda e, sem=sem, v=v: e.wait_ge(sem, v))

    def op(self, fn, *waits, inc=True):
        self.wait(*waits)
        if not inc:
            self.q.append(fn)
            return None
        self.n += 1
        self.q.append(lambda e: fn(e).then_inc(self.sem, 1))
        return (self.sem, self.n)

    def run(self, e):
        for f in self.q:
            f(e)


class Slot:

    def __init__(self, sem):
        self.sem, self.n = sem, 0

    def start(self, eng, out, in_, *waits):
        eng.wait(*waits)
        self.n += 16
        eng.q.append(lambda e: e.dma_start(out, in_).then_inc(self.sem, 16))
        return (self.sem, self.n)


class Ring:

    def __init__(self, n):
        self.n, self.i, self.free = n, -1, [[] for _ in range(n)]

    def take(self):
        self.i = (self.i + 1) % self.n
        return self.i, self.free[self.i]


def build(nc, x, W1, cw, dtb, alog, nw, Wo, cT, wmod, wg, cst, out):
    f32, f32r = mybir.dt.float32, mybir.dt.float32r
    ALU, ACT = mybir.AluOpType, mybir.ActivationFunctionType
    names = [0]

    def at(off, shape, dt=f32):
        names[0] += 1
        n = 4
        for s in shape[1:]:
            n *= s
        assert off % 32 == 0 and off + n <= 229216, (off, n)
        return nc.alloc_sbuf_tensor_at(f"t{names[0]}", shape, dt, offset=off)

    class Map:
        def __init__(self, base):
            self.p = base

        def new(self, shape, dt=f32):
            n = 4
            for s in shape[1:]:
                n *= s
            t = at(self.p, shape, dt)
            self.p += (n + 31) // 32 * 32
            return t

    scrU = nc.dram_tensor("scrU", (16, 128, 15, 128), f32).ap()
    scrA = nc.dram_tensor("scrA", (NS, 96, 32, 32), f32).ap()
    scrP = nc.dram_tensor("scrP", (NS, 96, 32, 32), f32).ap()
    scrX = nc.dram_tensor("scrX", (16, 128, D), f32).ap()

    M = Map(16384)
    NC_ = len(CONSTS) * 128
    cs = M.new([128, NC_ + 512 + 8])
    C = {n: cs[:, i * 128:(i + 1) * 128] for i, n in enumerate(CONSTS)}
    sel = cs[0:4, NC_:NC_ + 512]
    epsc, onec = cs[:, NC_ + 512:NC_ + 513], cs[:, NC_ + 513:NC_ + 514]
    ident = C["ident"]
    cwt = M.new([128, 12, 4])
    nwt = M.new([128, 1])
    dtbt, nexpA = M.new([128, H]), M.new([128, H])
    modT = M.new([128, 4, 4, NB])
    gnat = M.new([4, 2, D])
    g, nbeta, beta, nbg = (M.new([128, 16, H]) for _ in range(4))
    EX = M.new([128, NS, 4, 24])
    GC = M.new([128, NS, 2, NB, 3])
    mv, rs = M.new([128, 16, 2]), M.new([128, 16])
    st6 = M.new([128, 2, 6])
    kT = M.new([128, 3, NB * SEQ])
    P = M.new([128, NS, 24, 128])
    top = M.p
    A_ = Map(top)
    Hhi, Hlo = A_.new([128, 4, NB * SEQ], f32r), A_.new([128, 4, NB * SEQ], f32r)
    a_after_h = A_.p
    Wraw = [A_.new([128, 4, 128]) for _ in range(2)]
    Whi = [A_.new([128, 4, 128], f32r) for _ in range(2)]
    Wlo = [A_.new([128, 4, 128], f32r) for _ in range(2)]
    Y = [A_.new([128, SEQ]) for _ in range(2)]
    O = [A_.new([128, SEQ]) for _ in range(3)]
    Am = A_.new([128, 24, 128])
    GMT = A_.new([128, H, 128])
    EV = A_.new([128, H, 128])
    Ab = [A_.new([128, H, 128]) for _ in range(2)]
    nAp, Pp, tmp = A_.new([96, 32, 32]), A_.new([96, 32, 32]), A_.new([96, 256])
    assert A_.p <= 229216, A_.p
    p_off = top - NS * 24 * 128 * 4
    S_ = Map(p_off)
    wm = [S_.new([128, 4, 512]) for _ in range(2)]
    modn = S_.new([4, 6, 512])
    X = [S_.new([128, D]) for _ in range(3)]
    XN = [S_.new([128, D]) for _ in range(2)]
    HF = [S_.new([128, 4, 128]) for _ in range(1)]
    cTt = S_.new([128, 4, 4])
    sgn = S_.new([4, 2, D])
    assert S_.p <= top
    am_off = a_after_h + 11 * 2048
    ab = at(am_off, [12, NB * SEQ])
    zt = at(am_off + 8192, [128, 16, 12])
    z2 = at(am_off + 8192 + 768, [128, 16, H])
    z3 = at(am_off + 8192 + 768 + 384, [128, 16, H])
    B_ = Map(top)
    S = B_.new([128, NB * 3, 128])
    Sg = B_.new([128, 3, 128])
    U = [B_.new([128, 15, 128]) for _ in range(2)]
    GMb, Eb = B_.new([128, H, 128]), B_.new([128, H, 128])
    Kbg, Kd, Qg = B_.new([128, 3, 2, 64]), [B_.new([128, 3, 2, 64]) for _ in range(2)], B_.new([128, 3, 2, 64])
    Vb = [B_.new([128, H, 128]) for _ in range(2)]
    QgT, WT = [B_.new([128, 3, 128]) for _ in range(2)], [B_.new([128, 3, 128]) for _ in range(2)]
    PAn, PAT = B_.new([128, H, 128]), [B_.new([128, H, 128]) for _ in range(2)]
    dl = B_.new([128, H, 128])
    O2, Q2, R, OZ = B_.new([128, H, 128]), B_.new([128, 3, 128]), B_.new([128, H, 128]), B_.new([128, H, 128])
    XB = [B_.new([128, D]) for _ in range(2)]
    YB = [B_.new([128, D]) for _ in range(2)]
    Wot = B_.new([128, H, D])
    gaB = B_.new([128, NB, D])
    assert B_.p <= 229216, B_.p
    c0 = Map(p_off - 3 * NB * SEQ * 4)
    yacc = c0.new([128, 16, D])
    gbB = c0.new([128, NB, D])
    XC = [c0.new([128, D]) for _ in range(2)]
    xnc_off = c0.p
    XNC = [c0.new([128, D]) for _ in range(2)]
    GF = [at(xnc_off + i * 2048, [128, 512]) for i in range(2)]
    HFC = [c0.new([128, 4, 128]) for _ in range(1)]
    SI = [c0.new([128, 512]) for _ in range(2)]
    FH = [c0.new([128, 512], f32r) for _ in range(4)]
    FL = [c0.new([128, 512], f32r) for _ in range(4)]
    assert c0.p <= top, (c0.p, top)
    C_ = Map(a_after_h)
    Graw = C_.new([128, 3, 512])
    Ghi = [C_.new([128, 3, 512], f32r) for _ in range(4)]
    Glo = [C_.new([128, 3, 512], f32r) for _ in range(4)]
    assert C_.p <= 229216, C_.p

    PSt = nc.alloc_psum_tensor("ps", [128, 8, 512], f32)

    def bank(i):
        return PSt[:, i, :]

    def pair(i):
        return PSt[:, 2 * i:2 * i + 2, 0:384].rearrange("p a (m t) -> p a m t", m=3)

    def heads(t):
        return t.rearrange("p (a m) t -> p a m t", a=2)

    nsem = [0]

    def sem():
        nsem[0] += 1
        return nc.alloc_semaphore(f"s{nsem[0]}")

    PE, V, SC, G, SY = (Eng(sem()) for _ in range(5))

    def slots(n):
        return [Slot(sem()) for _ in range(n)]

    def bc(ap, axis, shape):
        return ap.unsqueeze(axis).broadcast_to(shape)

    def mm(o, l, r, start, stop, last=False, *waits):
        return PE.op(lambda e: e.matmul(o, l, r, start=start, stop=stop, skip_group_check=True), *waits, inc=last)

    def mm3(o, lh, ll, rh, rl, first, stop, last=False):
        mm(o, lh, rh, first, False)
        mm(o, ll, rh, False, False)
        return mm(o, lh, rl, False, stop, last)

    def tr(o, i, idn, last=False, *waits):
        return PE.op(lambda e: e.transpose(o, i, idn), *waits, inc=last)

    def act(o, i, f, *waits, **k):
        return SC.op(lambda e: e.activation(o, i, f, **k), *waits)

    def tt(E, o, a, b, op, *waits):
        return E.op(lambda e: e.tensor_tensor(o, a, b, op), *waits)

    def ts(E, o, a, s1, s2, o1, o2, *waits):
        if s2 is None:
            return E.op(lambda e: e.tensor_scalar(o, a, s1, None, o1), *waits)
        return E.op(lambda e: e.tensor_scalar(o, a, s1, s2, o1, o2), *waits)

    def stt(o, a, s, b, o1, o2, *waits):
        return V.op(lambda e: e.scalar_tensor_tensor(o, a, s, b, o1, o2), *waits)

    def cp(E, o, i, *waits):
        return E.op(lambda e: e.tensor_copy(o, i), *waits)

    SC.q.append(lambda e: e.preload_act_table_set("silu_and_others"))
    k_c, k_cw, k_nw, k_dt, k_al, k_cT = slots(6)
    t_cT = k_cT.start(SY, cTt[:, :, :], cT)
    t_cst = k_c.start(SY, cs[:, :], cst)
    wm_slots = slots(2)
    wm_ring = Ring(2)
    t_wm = []

    def load_mod(i):
        r, free = wm_ring.take()
        t_wm.append((r, wm_slots[r].start(SY, wm[r][:, :, :], wmod[:, :, i * 512:(i + 1) * 512], free)))

    load_mod(0)
    load_mod(1)
    t_cw = k_cw.start(SY, cwt[:, :, :], cw)
    t_nw = k_nw.start(SY, nwt[:, :], nw)
    t_dt = k_dt.start(SY, dtbt[:, :], dtb)
    t_al = k_al.start(SY, nexpA[:, :], alog)

    x_slots = slots(3)
    x_ring = Ring(3)

    def load_x(u):
        s, b = u // 4, u % 4
        r, free = x_ring.take()
        return r, x_slots[r].start(SY, X[r][:, :], x[b, s * 128:(s + 1) * 128, :], free)

    w_slots = slots(2)
    w_ring = Ring(2)
    wh_ring = Ring(2)

    def load_w(j):
        r, free = w_ring.take()
        return r, w_slots[r].start(SY, Wraw[r][:, :, :], W1[j], free)

    t_silu = act(cTt[:, :, :], cTt[:, :, :], ACT.Silu, t_cT)
    SC.q.append(lambda e: e.preload_act_table_set("natural_log_exp_and_others"))
    t_nexp0 = act(nexpA[:, :], nexpA[:, :], ACT.Exp, t_al)
    t_nexp = ts(V, nexpA[:, :], nexpA[:, :], -1.0, None, ALU.mult, None, t_nexp0)

    bfree = [[] for _ in range(8)]

    def split_w(j, ld):
        r, t = ld
        h, free = wh_ring.take()
        a = act(Whi[h][:, :, :], Wraw[r][:, :, :], ACT.Copy, t, free)
        b = tt(V, Wlo[h][:, :, :], Wraw[r][:, :, :], Whi[h][:, :, :].bitcast(f32), ALU.subtract, a, free)
        w_ring.free[r] = [b]
        return h, b

    def mod_rows(i):
        r, t = t_wm[i]
        bk = 4 + i % 2
        PE.wait(t, t_silu, bfree[bk])
        for k in range(4):
            tk = mm(bank(bk)[0:4, :], cTt[:, k, :], wm[r][:, k, :], k == 0, k == 3, k == 3)
        wm_ring.free[r] = [tk]
        if i in (1, 4):
            tm = ts(V, modn[:, i, :], bank(bk)[0:4, :], 1.0, None, ALU.add, None, tk)
        else:
            tm = cp(V, modn[:, i, :], bank(bk)[0:4, :], tk)
        bfree[bk] = [tm]
        return tm

    def mod_cols(i, dst, tm):
        PE.wait(tm, t_cst, bfree[6])
        for k in range(4):
            tk = tr(bank(6)[:, k * 4:k * 4 + 4], modn[:, i, k * 128:(k + 1) * 128], ident[0:4, 0:4], k == 3)
        t = cp(V, modT[:, dst, :, :].rearrange("p k b -> p (k b)"), bank(6)[:, 0:16], tk)
        bfree[6] = [t]
        return t

    m0, m1 = mod_rows(0), mod_rows(1)
    t_sa = mod_cols(0, 0, m0)
    t_ca = mod_cols(1, 1, m1)

    hf_free = [[], []]
    xn_free = [[], []]
    st_free = [[], []]

    def norm_to(u, src, t_src, XNs, HFs, i_sh, i_sc, t_mod, col):
        b = u % 4
        n = u % 2
        a = V.op(lambda e: e.bn_stats(st6[:, n, :], src), t_src, st_free[n])
        a = V.op(lambda e: e.bn_aggr(mv[:, u, :], st6[:, n, :]), a)
        st_free[n] = [a]
        l = act(rs[:, u:u + 1], mv[:, u, 1:2], ACT.Ln, a, bias=epsc)
        l = act(rs[:, u:u + 1], rs[:, u:u + 1], ACT.Exp, l, scale=-0.5)
        t_xn = ts(V, XNs[n][:, :], src, mv[:, u, 0:1], rs[:, u:u + 1], ALU.subtract, ALU.mult, l, xn_free[n])
        bk = 4 + n
        PE.wait(t_xn, bfree[bk])
        for k in range(4):
            tk = tr(bank(bk)[:, k * 128:(k + 1) * 128], XNs[n][:, k * 128:(k + 1) * 128], ident, k == 3)
        xn_free[n] = [tk]
        m = len(HFs) - 1 and n
        for k in range(4):
            t_h = ts(V, HFs[m][:, k, :], bank(bk)[:, k * 128:(k + 1) * 128], modT[:, i_sc, k, b:b + 1],
                     modT[:, i_sh, k, b:b + 1], ALU.mult, ALU.add, tk, t_mod, hf_free[m])
        bfree[bk] = [t_h]
        hi = act(Hhi[:, :, col:col + 128], HFs[m][:, :, :], ACT.Copy, t_h)
        lo = tt(V, Hlo[:, :, col:col + 128], HFs[m][:, :, :], Hhi[:, :, col:col + 128].bitcast(f32), ALU.subtract, hi)
        hf_free[m] = [lo]
        return t_xn, lo

    t_hn = {}
    order = [s * 4 + b for b in range(4) for s in range(4)]
    xl = [load_x(order[0]), load_x(order[1])]
    wl = [load_w(0), load_w(1)]
    for n, u in enumerate(order):
        if n + 2 < 16:
            xl.append(load_x(order[n + 2]))
        s, b = u // 4, u % 4
        r, t = xl[n]
        tx, t_hn[u] = norm_to(u, X[r][:, :], t, XN, HF, 0, 1, [t_sa, t_ca, t_cst], b * SEQ + s * 128)
        x_ring.free[r] = [tx]
    t_hb = [t_hn[12 + b] for b in range(4)]
    load_mod(2)
    load_mod(3)

    def late_mods(early):
        tms = early + [mod_rows(4), mod_rows(5)]
        t_sb, t_cb = mod_cols(3, 2, tms[1]), mod_cols(4, 3, tms[2])
        for n, i in ((0, 2), (1, 5)):
            src = modn[:, i, :]
            a = stt(gnat[:, n, :], src, -1.0, src, ALU.mult, ALU.max, tms[i - 2])
            a = ts(V, gnat[:, n, :], gnat[:, n, :], 0.25, None, ALU.max, None, a)
            c_ = ts(V, sgn[:, n, :], src, 0.0, 2.0, ALU.is_ge, ALU.mult, a)
            c_ = ts(V, sgn[:, n, :], sgn[:, n, :], -1.0, None, ALU.add, None, c_)
            t = tt(V, gnat[:, n, :], gnat[:, n, :], sgn[:, n, :], ALU.mult, c_)
        return t_sb, t_cb, t

    pr = Ring(4)

    def project(h, tw, b):
        i, free = pr.take()
        PE.wait(free, tw, t_hb[b])
        c = slice(b * SEQ, (b + 1) * SEQ)
        for k in range(4):
            t = mm3(bank(i), Whi[h][:, k, :], Wlo[h][:, k, :], Hhi[:, k, c], Hlo[:, k, c], k == 0, k == 3, k == 3)
        return i, t

    y_ring, o_ring = Ring(2), Ring(3)
    o_slots = slots(3)

    def conv(i, t, j):
        y, free = y_ring.take()
        p, yy = bank(i), Y[y]
        w = lambda n: cwt[:, j, n:n + 1]
        a = act(yy[:, :], p, ACT.Copy, t, free, t_cw, scale=w(3))
        for n in (2, 1, 0):
            d = 3 - n
            a = stt(yy[:, d:SEQ], p[:, 0:SEQ - d], w(n), yy[:, d:SEQ], ALU.mult, ALU.add, a)
        pr.free[i] = [a]
        return y, a

    t_scrU = {}

    def store_unit(o, t, tile, b):
        dst = scrU.rearrange("(s b) p j t -> b j p s t", b=4)[b, tile]
        src = O[o][:, :].rearrange("p (s t) -> p s t", s=4)
        tk = o_slots[o].start(SY, dst, src, t)
        o_ring.free[o] = [tk]
        t_scrU[(tile, b)] = tk

    def next_w(j):
        got_w = split_w(j, wl[j])
        if j + 2 < NT1:
            wl.append(load_w(j + 2))
        return got_w

    h, tw = next_w(0)
    for b in range(4):
        i, t = project(h, tw, b)
        t_ab = cp(V, ab[:, b * SEQ:(b + 1) * SEQ], bank(i)[0:12, :], t)
        pr.free[i] = [t_ab]
    wh_ring.free[h] = [t]
    t_k = {}
    SC.q.append(lambda e: e.preload_act_table_set("silu_and_others"))
    for m in range(3):
        h, tw = next_w(1 + m)
        for b in range(4):
            i, t = project(h, tw, b)
            y, a = conv(i, t, m)
            t_k[(m, b)] = act(kT[:, m, b * SEQ:(b + 1) * SEQ], Y[y][:, :], ACT.Silu, a)
            y_ring.free[y] = [t_k[(m, b)]]
        wh_ring.free[h] = [t]
        if m == 0:
            early = [mod_rows(2), mod_rows(3)]
            load_mod(4)
            load_mod(5)
    t_sb, t_cb, t_gn = late_mods(early)
    PE.wait(t_ab, t_cst, bfree[7])
    for u in range(16):
        s, b = u // 4, u % 4
        tk = tr(bank(7)[:, u * 12:u * 12 + 12], ab[:, b * SEQ + s * 128:b * SEQ + s * 128 + 128],
                ident[0:12, 0:12], u == 15)
    t_z = cp(V, zt[:, :, :].rearrange("p u c -> p (u c)"), bank(7)[:, 0:192], tk)
    bfree[7] = [t_z]
    SC.q.append(lambda e: e.preload_act_table_set("natural_log_exp_and_others"))
    sh = [128, 16, H]
    t_a = tt(V, zt[:, :, 0:6], zt[:, :, 0:6], bc(dtbt[:, :], 1, sh), ALU.add, t_z, t_dt)
    a = act(z2[:, :, :], zt[:, :, 0:6], ACT.Abs, t_a)
    a = act(z2[:, :, :], z2[:, :, :], ACT.Exp, a, scale=-1.0)
    a = act(z2[:, :, :], z2[:, :, :], ACT.Ln, a, bias=onec)
    a = stt(z3[:, :, :], zt[:, :, 0:6], 0.0, z2[:, :, :], ALU.max, ALU.add, a)
    t_g = tt(V, g[:, :, :], z3[:, :, :], bc(nexpA[:, :], 1, sh), ALU.mult, a, t_nexp)
    a = act(z2[:, :, :], zt[:, :, 6:12], ACT.Exp, a, scale=-1.0)
    a = ts(V, z2[:, :, :], z2[:, :, :], 1.0, None, ALU.add, None, a)
    t_be = V.op(lambda e: e.reciprocal(beta[:, :, :], z2[:, :, :]), a)
    t_nb = ts(V, nbeta[:, :, :], beta[:, :, :], -1.0, None, ALU.mult, None, t_be)
    nk = 0
    t_kn = {}
    sq_free = [[], []]
    for b in range(4):
        for m in range(3):
            c = slice(b * SEQ, (b + 1) * SEQ)
            bk = 4 + nk % 2
            yb = nk % 2
            nk += 1
            a = tt(G, Y[yb][:, :], kT[:, m, c], kT[:, m, c], ALU.mult, t_k[(m, b)], sq_free[yb], y_ring.free[yb])
            t = mm(bank(bk), C["BO"], Y[yb][:, :], True, True, True, a, bfree[bk])
            a = act(Y[yb][:, :], bank(bk), ACT.Ln, t)
            bfree[bk] = [a]
            a = act(Y[yb][:, :], Y[yb][:, :], ACT.Exp, a, scale=-0.5)
            t_kn[(m, b)] = tt(V, kT[:, m, c], kT[:, m, c], Y[yb][:, :], ALU.mult, a)
            sq_free[yb] = [t_kn[(m, b)]]
            y_ring.free[yb] = [t_kn[(m, b)]]
    t_kb = [t_kn[(2, b)] for b in range(4)]
    t_p0 = G.op(lambda e: e.memset(P[:, :, :, :], 0.0), t_hb, xn_free, hf_free, t_sb, t_cb, t_gn)

    pairs = Ring(2)
    pairs.free = [[bfree[4], bfree[5]], [bfree[6], bfree[7]]]

    def pfree(i, t):
        pairs.free[i] = [t]

    ab_ring = Ring(2)
    a_slots = [slots(4), slots(4)]
    am_free = []
    gm_free, ev_free = [], []
    t_ex = {}

    def decay_rows(s, b, GMx, Ex, free_gm, free_e):
        u = s * 4 + b
        a = tt(V, GMx[:, :, :], bc(C["SG"], 1, [128, H, 128]), bc(g[:, u, :], 2, [128, H, 128]), ALU.mult,
               t_g, free_gm)
        p, free = pairs.take()
        PE.wait(a, free)
        for par in range(2):
            t = mm(PSt[:, 4 + 2 * p + par, 0:384], C["LE"], GMx[:, 3 * par:3 * par + 3, :], True, True, par == 1)
        e = act(heads(Ex[:, :, :]), pair(2 + p), ACT.Exp, t, free_e)
        pfree(p, e)
        return t, e

    def sums(s):
        p, free = pairs.take()
        bk = bank(4 + 2 * p)
        rhs = g[:, 4 * s:4 * s + 4, :].rearrange("p u h -> p (u h)")
        PE.wait(free, t_g)
        for n, w in enumerate(("LE", "SG", "CH0", "CH1")):
            t = mm(bk[:, n * 24:n * 24 + 24], C[w], rhs, n == 0, True, n == 3)
        e = act(EX[:, s, :, :].rearrange("p n h -> p (n h)"), bk[:, 0:96], ACT.Exp, t)
        pfree(p, e)
        v = EX[:, s, :, :].rearrange("p n (b a m) -> p n b a m", b=4, a=2)
        for par in range(2):
            q = slice(64 * par, 64 * par + 64)
            for c in range(2):
                a = cp(V, GC[q, s, c, :, :], v[q, 2 + c, :, par, :], e)
        w = tt(V, nbg[:, 4 * s:4 * s + 4, :].rearrange("p u h -> p (u h)"),
               nbeta[:, 4 * s:4 * s + 4, :].rearrange("p u h -> p (u h)"), EX[:, s, 0, :], ALU.mult, e, t_nb)
        t_ex[s] = w

    def inverse_1(s):
        nonlocal am_free, gm_free, ev_free
        sums(s)
        toks = []
        am = []
        for b in range(4):
            u = s * 4 + b
            gm, e = decay_rows(s, b, GMT, EV, gm_free, ev_free)
            gm_free = [gm]
            p, free = pairs.take()
            PE.wait(free, t_kb[b])
            for m in range(3):
                for par in range(2):
                    r = slice(64 * par, 64 * par + 64)
                    kk = kT[r, m, b * SEQ + s * 128:b * SEQ + s * 128 + 128]
                    t = mm(PSt[:, 4 + 2 * p + par, m * 128:m * 128 + 128], kk, kk, True, True, m == 2 and par == 1)
            i, free = ab_ring.take()
            a = tt(V, heads(Ab[i][:, :, :]), pair(2 + p), heads(EV[:, :, :]), ALU.mult, t, e, free)
            pfree(p, a)
            ev_free = [a]
            a = tt(G, Ab[i][:, :, :], Ab[i][:, :, :], bc(nbeta[:, u, :], 2, [128, H, 128]), ALU.mult, a, t_nb)
            am.append(tt(G, Am[:, b * 6:b * 6 + 6, :], Ab[i][:, :, :], bc(C["LL"], 1, [128, H, 128]), ALU.mult,
                         a, am_free))
            d = []
            for k in range(4):
                q = slice(32 * k, 32 * k + 32)
                d.append(a_slots[i][k].start(G, scrA[s, k * 24 + b * 6:k * 24 + b * 6 + 6].rearrange("h t i -> t h i"),
                                             Ab[i][q, :, q], a))
            ab_ring.free[i] = [am[-1]] + d
            toks += d
        return toks, am

    nap_slot, pp_slot = slots(1)[0], slots(1)[0]
    pin_slots = slots(4)
    pool_free = []

    def inverse_2(s, toks):
        nonlocal pool_free
        t = nap_slot.start(G, nAp[:, :, :], scrA[s], toks, pool_free)
        a = G.op(lambda e: e.memset(Pp[:, :, :], 0.0), pool_free)
        dg = Pp[:, :, :].rearrange("p a b -> p (a b)")[:, 0:1024:33]
        a = G.op(lambda e: e.memset(dg, 1.0), a)
        G.wait(t)
        for j in range(31):
            n, w = j + 1, 31 - j
            tm = tmp[:, 0:n * w].rearrange("p (c t) -> p c t", c=n)
            a = tt(G, tm, Pp[:, 0:n, j:j + 1].broadcast_to([96, n, w]),
                   bc(nAp[:, j + 1:32, j], 1, [96, n, w]), ALU.mult, a)
            a = tt(G, Pp[:, 0:n, j + 1:32], Pp[:, 0:n, j + 1:32], tm, ALU.add, a)
        o = pp_slot.start(G, scrP[s], Pp[:, :, :], a)
        pool_free = [o]
        d = []
        for k in range(4):
            q = slice(32 * k, 32 * k + 32)
            d.append(pin_slots[k].start(G, P[q, s, :, q], scrP[s, k * 24:k * 24 + 24].rearrange("h c t -> c h t"),
                                        o, t_p0))
        return d

    t_P = {}

    def merge(s, din, am):
        nonlocal am_free, gm_free, ev_free
        am_free = []
        for b in range(4):
            hb = slice(b * 6, b * 6 + 6)
            tT = V.op(lambda e, hb=hb: e.transpose(GMT[:, :, :], P[:, s, hb, :]), din, gm_free)
            p, free = pairs.take()
            PE.wait(free, din, am[b])
            for h_ in range(6):
                t = mm(PSt[:, 4 + 2 * p + h_ // 3, (h_ % 3) * 128:(h_ % 3) * 128 + 128], Am[:, b * 6 + h_, :],
                       P[:, s, b * 6 + h_, :], True, True, h_ == 5)
            am_free.append(t)
            v = act(heads(EV[:, :, :]), pair(2 + p), ACT.Copy, t, ev_free)
            pfree(p, v)
            p, free = pairs.take()
            PE.wait(free, v, tT)
            for h_ in range(6):
                t2 = mm(PSt[:, 4 + 2 * p + h_ // 3, (h_ % 3) * 128:(h_ % 3) * 128 + 128], GMT[:, h_, :],
                        EV[:, h_, :], True, True, h_ == 5)
            gm_free, ev_free = [t2], [t2]
            for c in range(2):
                q, w = slice(64 * c, 64 * c + 32), slice(64 * c + 32, 64 * c + 64)
                a = cp(V, heads(P[:, s, hb, :])[q, :, :, w], pair(2 + p)[q, :, :, w], t2, tT)
            pfree(p, a)
            t_P[(s, b)] = a

    tiles = [("q", m) for m in range(3)] + [("v", h_) for h_ in range(6)] + [("g", h_) for h_ in range(6)]
    plan = {0: ("i", 0), 4: ("m", 0), 5: ("i", 1), 8: ("m", 1), 9: ("i", 2), 12: ("m", 2), 13: ("i", 3)}
    late = None
    din, ams = {}, {}
    cur = None
    for n, (kind, m) in enumerate(tiles):
        h, tw = next_w(4 + n)
        if kind != "k" and cur != "silu":
            SC.q.append(lambda e: e.preload_act_table_set("silu_and_others"))
            cur = "silu"
        for b in range(4):
            i, t = project(h, tw, b)
            o, free = o_ring.take()
            if kind == "g":
                a = act(O[o][:, :], bank(i), ACT.Silu, t, free)
                pr.free[i] = [a]
                a = ts(G, O[o][:, :], O[o][:, :], nwt[:, 0:1], None, ALU.mult, None, a, t_nw)
            else:
                y, a = conv(i, t, 3 + n)
                a = act(O[o][:, :], Y[y][:, :], ACT.Silu, a, free)
                y_ring.free[y] = [a]
            store_unit(o, a, n, b)
        wh_ring.free[h] = [t]
        if n in plan:
            k, s = plan[n]
            SC.q.append(lambda e: e.preload_act_table_set("natural_log_exp_and_others"))
            cur = "exp"
            if k == "i":
                tk, ams[s] = inverse_1(s)
                din[s] = inverse_2(s, tk)
            else:
                merge(s, din[s], ams[s])
    SC.q.append(lambda e: e.preload_act_table_set("natural_log_exp_and_others"))
    merge(3, din[3], ams[3])

    a_done = [t, a, o_ring.free, am_free, gm_free, ev_free, pool_free, wh_ring.free, y_ring.free]
    p_ready = [t_P[(3, 3)], (V.sem, V.n), (PE.sem, PE.n), (SC.sem, SC.n), (G.sem, G.n)]
    stores = [t_scrU[k] for k in t_scrU]
    allA = p_ready + [o_ring.free]
    t_wo = slots(1)[0].start(SY, Wot[:, :, :], Wo, allA, stores)
    u_slots, u_ring = slots(2), Ring(2)
    xb_slots, xb_ring = slots(2), Ring(2)
    PE.wait(allA)
    V.wait(allA)
    SC.wait(allA)
    G.wait(allA)
    t_s0 = V.op(lambda e: e.memset(S[:, :, :], 0.0))
    t_d0 = V.op(lambda e: e.memset(dl[:, :, :], 0.0))

    def gate_rows(n, dst):
        for b in range(NB):
            p, free = pairs.take()
            bk = bank(4 + 2 * p)
            t = mm(bk, sel[:, b * 128:(b + 1) * 128], gnat[:, n, :], True, True, True, free, t_gn)
            a = act(dst[:, b, :], bk, ACT.Copy, t)
            pfree(p, a)
        return a

    t_ga = gate_rows(0, gaB)

    gmb_free, eb_free, kbg_free, qg_free, pan_free = [], [], [], [], []
    r2 = {n: Ring(2) for n in ("Kd", "Vb", "QgT", "WT", "PAT")}
    dfree, ofree = [bfree[0], bfree[1], pr.free[0], pr.free[1]], [bfree[2], bfree[3], pr.free[2], pr.free[3]]
    t_S, S_read = {}, {}
    for b in range(4):
        t_S[b] = t_s0

    def load_u(u):
        r, free = u_ring.take()
        return r, u_slots[r].start(SY, U[r][:, :, :], scrU[u], allA, stores, free)

    ul = [load_u(0), load_u(1)]
    got = {}

    def prep(u):
        nonlocal gmb_free, eb_free, kbg_free, qg_free, pan_free
        s, b = u // 4, u % 4
        r, t_u = ul[u]
        col = slice(b * SEQ + s * 128, b * SEQ + s * 128 + 128)
        sc_ = lambda ap: bc(ap.rearrange("p (a m) -> p m a", a=2), 3, [128, 3, 2, 64])
        ex = lambda n: EX[:, s, n, b * 6:b * 6 + 6]
        q3 = lambda bk: bk[:, 0:384].rearrange("p (m a t) -> p m a t", m=3, a=2)
        o = {"r": r, "t_u": t_u}
        p, free = pairs.take()
        PE.wait(free, t_u)
        for m in range(3):
            tr(bank(4 + 2 * p)[:, m * 128:m * 128 + 128], kT[:, m, col], ident)
        for m in range(3):
            t = tr(bank(5 + 2 * p)[:, m * 128:m * 128 + 128], U[r][:, m, :], ident, m == 2)
        n_, free = r2["Kd"].take()
        o["Kd"] = n_
        o["t_kbg"] = tt(V, Kbg[:, :, :, :], q3(bank(4 + 2 * p)), sc_(nbg[:, u, :]), ALU.mult, t, kbg_free)
        o["t_kd"] = tt(V, Kd[n_][:, :, :, :], q3(bank(4 + 2 * p)), sc_(ex(1)), ALU.mult, free)
        t_qg = tt(V, Qg[:, :, :, :], q3(bank(5 + 2 * p)), sc_(ex(0)), ALU.mult, qg_free)
        pfree(p, t_qg)
        yield
        p, free = pairs.take()
        PE.wait(free)
        for h_ in range(6):
            t = tr(PSt[:, 4 + 2 * p + h_ // 3, (h_ % 3) * 128:(h_ % 3) * 128 + 128], U[r][:, 3 + h_, :], ident, h_ == 5)
        n_, free = r2["Vb"].take()
        o["Vb"] = n_
        o["t_vb"] = tt(V, heads(Vb[n_][:, :, :]), pair(2 + p),
                       bc(beta[:, u, :].rearrange("p (a m) -> p a m", a=2), 3, [128, 2, 3, 128]), ALU.mult, t, free)
        pfree(p, o["t_vb"])
        yield
        gm, e = decay_rows(s, b, GMb, Eb, gmb_free, eb_free)
        gmb_free = [gm]
        yield
        p, free = pairs.take()
        PE.wait(free, t_qg, o["t_kbg"], t_P[(s, b)])
        for m in range(3):
            t1 = tr(bank(4 + 2 * p)[:, m * 128:m * 128 + 128], Qg[:, m, :, :].rearrange("p a t -> p (a t)"), ident)
        for m in range(3):
            for par in range(2):
                t = mm(PSt[64 * par:64 * par + 64, 5 + 2 * p, m * 128:m * 128 + 128], Kbg[:, m, par, :],
                       P[:, s, b * 6 + par * 3 + m, :], True, True, m == 2 and par == 1)
        kbg_free, qg_free = [t], [t]
        n_, free = r2["QgT"].take()
        o["QgT"] = n_
        act(QgT[n_][:, :, :].rearrange("p m t -> p (m t)"), bank(4 + 2 * p)[:, 0:384], ACT.Copy, t, free)
        n_, free = r2["WT"].take()
        o["WT"] = n_
        o["t_wt"] = act(WT[n_][:, :, :].rearrange("p m t -> p (m t)"), bank(5 + 2 * p)[:, 0:384], ACT.Copy, free)
        pfree(p, o["t_wt"])
        yield
        p, free = pairs.take()
        PE.wait(free)
        for m in range(3):
            for par in range(2):
                q = slice(64 * par, 64 * par + 64)
                t = mm(PSt[:, 4 + 2 * p + par, m * 128:m * 128 + 128], U[r][q, m, :], kT[q, m, col], True, True,
                       m == 2 and par == 1)
        a = tt(V, heads(PAn[:, :, :]), pair(2 + p), heads(Eb[:, :, :]), ALU.mult, t, e, pan_free)
        pfree(p, a)
        eb_free = [a]
        p, free = pairs.take()
        PE.wait(free, a)
        for h_ in range(6):
            t = tr(PSt[:, 4 + 2 * p + h_ // 3, (h_ % 3) * 128:(h_ % 3) * 128 + 128], PAn[:, h_, :], ident, h_ == 5)
        pan_free = [t]
        n_, free = r2["PAT"].take()
        o["PAT"] = n_
        le = C["LE"].unsqueeze(1).unsqueeze(1).broadcast_to([128, 2, 3, 128])
        o["t_pat"] = tt(V, heads(PAT[n_][:, :, :]), pair(2 + p), le, ALU.mult, t, free)
        pfree(p, o["t_pat"])
        got[u] = o
        yield

    dl_w = [[t_d0], [t_d0]]
    dl_r = [[], []]
    sg_free = []

    def rec(u):
        nonlocal dfree, ofree, sg_free
        s, b = u // 4, u % 4
        o = got[u]
        kd, vb, qg, wt, pa = Kd[o["Kd"]], Vb[o["Vb"]], QgT[o["QgT"]], WT[o["WT"]], PAT[o["PAT"]]
        PE.wait(dfree, o["t_vb"], t_P[(s, b)], o["t_wt"])
        for m in range(3):
            for par in range(2):
                h_ = par * 3 + m
                mm(PSt[:, par, m * 128:m * 128 + 128], P[:, s, b * 6 + h_, :], vb[:, h_, :], m == 0, True)
        for c in range(2):
            q = slice(64 * c, 64 * c + 64)
            PE.wait(t_S[b])
            for m in range(3):
                for par in range(2):
                    w = slice(64 * par, 64 * par + 64)
                    t = mm(PSt[q, par, m * 128:m * 128 + 128], wt[w, m, q], S[w, b * 3 + m, :], False, True,
                           m == 2 and par == 1)
            t_dl = act(heads(dl[:, :, :])[q], pair(0)[q], ACT.Copy, t, dl_w[c], dl_r[0], dl_r[1])
            gcv = GC[:, s, c, b, :]
            t_sg = tt(G, Sg[:, :, :], S[:, b * 3:b * 3 + 3, :], bc(gcv, 2, [128, 3, 128]), ALU.mult, t_S[b], sg_free,
                      t_ex[s])
            if c == 0:
                PE.wait(ofree)
            for m in range(3):
                for par in range(2):
                    w = slice(64 * par, 64 * par + 64)
                    t_o1 = mm(PSt[:, 2 + par, m * 128 + 64 * c:m * 128 + 64 * c + 64], S[w, b * 3 + m, :],
                              qg[w, m, q], c == 0 and m == 0, True, m == 2 and par == 1)
            yield
            p, free = pairs.take()
            PE.wait(free, t_dl, o["t_kd"], o["t_pat"])
            for m in range(3):
                for par in range(2):
                    w = slice(64 * par, 64 * par + 64)
                    t_s = mm(PSt[w, 4 + 2 * p, m * 128:m * 128 + 128], kd[q, m, par, :], dl[q, par * 3 + m, :],
                             True, True, m == 2 and par == 1)
            a = tt(V, S[:, b * 3:b * 3 + 3, :], Sg[:, :, :],
                   bank(4 + 2 * p)[:, 0:384].rearrange("p (m t) -> p m t", m=3), ALU.add, t_s, t_sg, t_o1)
            t_S[b] = a
            sg_free = [a]
            pfree(p, a)
            for m in range(3):
                for par in range(2):
                    h_ = par * 3 + m
                    t_o = mm(PSt[:, 2 + par, m * 128 + 64 * c:m * 128 + 64 * c + 64], dl[:, h_, :], pa[:, h_, q],
                             False, True, m == 2 and par == 1)
            dl_r[c] = [t_o]
            yield
        dfree = [t_dl]
        o["t_o"] = t_o
        r2["Kd"].free[o["Kd"]] = [t_o]
        r2["Vb"].free[o["Vb"]] = [t_o]
        r2["QgT"].free[o["QgT"]] = [t_o]
        r2["WT"].free[o["WT"]] = [t_o]
        r2["PAT"].free[o["PAT"]] = [t_o]

    o2_free, q2_free, oz_free = [], [], []
    rr_free = []
    x1_slots, x1_ring = slots(2), Ring(2)
    xbl = {}

    def load_xb(u):
        s, b = u // 4, u % 4
        r, free = xb_ring.take()
        xbl[u] = (r, xb_slots[r].start(SY, XB[r][:, :], x[b, s * 128:(s + 1) * 128, :], allA, free))

    load_xb(0)
    load_xb(1)
    t_x1 = {}
    ho = lambda t: t[:, :, :].rearrange("p (a m) t -> p a (m t)", a=2)

    def post(u):
        nonlocal ofree, o2_free, q2_free, oz_free, rr_free
        s, b = u // 4, u % 4
        o = got[u]
        r = o["r"]
        op = PSt[:, 2:4, 0:384]
        a = act(ho(O2), op, ACT.Square, o["t_o"], o2_free)
        q = tt(G, Q2[:, :, :], U[r][:, 0:3, :], U[r][:, 0:3, :], ALU.mult, o["t_u"], q2_free)
        p, free = pairs.take()
        PE.wait(free, a, q)
        for par in range(2):
            mm(PSt[:, 4 + 2 * p + par, 0:384], C["ON"], O2[:, 3 * par:3 * par + 3, :], True, False)
        for par in range(2):
            w = slice(64 * par, 64 * par + 64)
            t = mm(PSt[:, 4 + 2 * p + par, 0:384], C["EP"][w, :], Q2[w, :, :], False, True, par == 1)
        o2_free, q2_free = [t], [t]
        a = act(ho(R), PSt[:, 4 + 2 * p:6 + 2 * p, 0:384], ACT.Ln, t, rr_free)
        pfree(p, a)
        a = act(R[:, :, :], R[:, :, :], ACT.Exp, a, scale=-0.5)
        a = tt(V, ho(OZ), op, ho(R), ALU.mult, a, oz_free)
        ofree = [a]
        rr_free = [a]
        a = tt(G, OZ[:, :, :], OZ[:, :, :], U[r][:, 9:15, :], ALU.mult, a)
        u_ring.free[r] = [a, o["t_o"], t]
        if u + 2 < 16:
            ul.append(load_u(u + 2))
        yield
        p, free = pairs.take()
        PE.wait(free, a, t_wo)
        for h_ in range(6):
            t = mm(bank(4 + 2 * p), OZ[:, h_, :], Wot[:, h_, :], h_ == 0, h_ == 5, h_ == 5)
        oz_free = [t]
        xr, t_x = xbl[u]
        k, free = x1_ring.take()
        a = tt(V, YB[k][:, :], bank(4 + 2 * p), gaB[:, b, :], ALU.mult, t, t_ga, free)
        pfree(p, a)
        a = tt(G, YB[k][:, :], YB[k][:, :], XB[xr][:, :], ALU.add, a, t_x)
        xb_ring.free[xr] = [a]
        t_x1[u] = x1_slots[k].start(SY, scrX[u], YB[k][:, :], a)
        x1_ring.free[k] = [t_x1[u]]
        if u + 2 < 16:
            load_xb(u + 2)
        yield

    def weave(*gens):
        gens = [g_ for g_ in gens if g_ is not None]
        while gens:
            for g_ in list(gens):
                if next(g_, "end") == "end":
                    gens.remove(g_)

    weave(prep(0))
    for u in range(16):
        weave(rec(u), prep(u + 1) if u < 15 else None)
        weave(post(u))

    allB = [(E_.sem, E_.n) for E_ in (PE, V, SC, G)] + [x1_ring.free, xb_ring.free, u_ring.free]
    for E_ in (PE, V, SC, G, SY):
        E_.wait(allB)
    hf_free[:] = [[], []]
    xn_free[:] = [[], []]
    bfree[:] = [[] for _ in range(8)]
    pairs.free = [[], []]
    t_gb = gate_rows(1, gbB)
    bfree[4], bfree[6] = pairs.free[0], pairs.free[1]
    xc_slots, xc_ring = slots(2), Ring(2)

    def load_xc(u, *w):
        r, free = xc_ring.take()
        return r, xc_slots[r].start(SY, XC[r][:, :], scrX[u], t_x1[u], free, *w)

    graw_slot = slots(1)[0]
    graw_free = []
    gw = Ring(4)

    def load_ff(j):
        nonlocal graw_free
        t = graw_slot.start(SY, Graw[:, :, :], wg[j], graw_free)
        r, free = gw.take()
        a = act(Ghi[r][:, :, :], Graw[:, :, :], ACT.Copy, t, free)
        b_ = tt(V, Glo[r][:, :, :], Graw[:, :, :], Ghi[r][:, :, :].bitcast(f32), ALU.subtract, a, free)
        graw_free = [b_]
        return r, b_

    orderc = [s * 4 + b for b in range(4) for s in range(4)]
    xl = [load_xc(orderc[0]), load_xc(orderc[1])]
    fw = {0: load_ff(0), 1: load_ff(1)}
    t_hc = {}
    done_n = 0

    def norm_batch(b):
        for s in range(4):
            u = s * 4 + b
            n = b * 4 + s
            if n >= 2:
                xl.append(load_xc(u))
            r, t = xl[n]
            tx, t_hc[u] = norm_to(u, XC[r][:, :], t, XNC, HFC, 2, 3, [t_sb, t_cb], b * SEQ + s * 128)
            xc_ring.free[r] = [tx]

    SC.q.append(lambda e: e.preload_act_table_set("natural_log_exp_and_others"))
    for b in range(4):
        norm_batch(b)
    SC.q.append(lambda e: e.preload_act_table_set("silu_and_others"))
    gub = Ring(4)
    yb = Ring(4)
    yb.free = [[bfree[4]], [bfree[5]], [bfree[6]], [bfree[7]]]
    si_ring, gf_ring, f_ring = Ring(2), Ring(2), Ring(4)
    xo_slots = slots(2)
    t_y = {}
    outs = []
    NG = 8
    for q in range(NG):
        for b in range(4):
            if b == 2 and q + 1 < NG:
                pass
            c = slice(b * SEQ, (b + 1) * SEQ)
            fs = []
            for jj in range(2):
                j = 2 * q + jj
                w, tw = fw[j]
                i1, free1 = gub.take()
                i2, free2 = gub.take()
                PE.wait(free1, free2, tw, t_hc[12 + b])
                for n, i in ((0, i1), (1, i2)):
                    for k in range(4):
                        kk = slice(k * 128, (k + 1) * 128)
                        t = mm3(bank(i), Ghi[w][:, n, kk], Glo[w][:, n, kk], Hhi[:, k, c], Hlo[:, k, c], k == 0,
                                k == 3, k == 3)
                    if n == 0:
                        z, free = si_ring.take()
                        t_si = act(SI[z][:, :], bank(i), ACT.Silu, t, free)
                        gub.free[i] = [t_si]
                f, free = gf_ring.take()
                a = tt(V, GF[f][:, :], bank(i2), SI[z][:, :], ALU.mult, t, t_si, free)
                gub.free[i2] = [a]
                si_ring.free[z] = [a]
                k, free = f_ring.take()
                hi = act(FH[k][:, :], GF[f][:, :], ACT.Copy, a, free)
                lo = tt(V, FL[k][:, :], GF[f][:, :], FH[k][:, :].bitcast(f32), ALU.subtract, hi, free)
                gf_ring.free[f] = [lo]
                fs.append((k, w, lo))
            for s in range(4):
                u = s * 4 + b
                i, free = yb.take()
                PE.wait(free, fs[0][2], fs[1][2])
                for n, (k, w, _) in enumerate(fs):
                    tk = slice(s * 128, (s + 1) * 128)
                    t = mm3(bank(4 + i), FH[k][:, tk], FL[k][:, tk], Ghi[w][:, 2, :], Glo[w][:, 2, :], n == 0, n == 1,
                            n == 1)
                if q == 0:
                    t_y[u] = cp(V, yacc[:, u, :], bank(4 + i), t)
                else:
                    t_y[u] = tt(V, yacc[:, u, :], bank(4 + i), yacc[:, u, :], ALU.add, t, t_y[u])
                yb.free[i] = [t_y[u]]
                if q == NG - 1:
                    r, t_x = load_xc(u)
                    a = tt(G, yacc[:, u, :], yacc[:, u, :], gbB[:, b, :], ALU.mult, t_y[u], t_gb)
                    a = tt(G, yacc[:, u, :], yacc[:, u, :], XC[r][:, :], ALU.add, a, t_x)
                    xc_ring.free[r] = [a]
                    outs.append(xo_slots[0] if 0 else Slot(sem()))
                    outs[-1] = outs[-1].start(SC, out[b, s * 128:(s + 1) * 128, :], yacc[:, u, :], a)
            for k, w, _ in fs:
                f_ring.free[k] = [t]
        for k, w, _ in fs:
            gw.free[w] = [t]
        if q == 0:
            fw[2], fw[3] = load_ff(2), load_ff(3)
        if 2 * q + 5 < 16:
            fw[2 * q + 4], fw[2 * q + 5] = load_ff(2 * q + 4), load_ff(2 * q + 5)
    SY.wait(outs)

    with nc.Block() as block:
        @block.sync
        def _(e):
            SY.run(e)

        @block.tensor
        def _(e):
            PE.run(e)

        @block.vector
        def _(e):
            V.run(e)

        @block.scalar
        def _(e):
            SC.run(e)

        @block.gpsimd
        def _(e):
            G.run(e)


def tiles(w, n):
    return np.ascontiguousarray(w.reshape(4, 128, n, 128).transpose(2, 1, 0, 3))


def kernel(**inputs):
    import concourse.bacc as bacc
    from concourse.bass_utils import run_bass_kernel_spmd

    v = {k: np.asarray(a) for k, a in inputs.items()}
    A = lambda n: v["L0_attn_" + n]
    wab = np.zeros((D, 128), np.float32)
    wab[:, 0:6] = A("Wa")[:, HEADS]
    wab[:, 6:12] = A("Wb")[:, HEADS]
    hv = lambda w: w.reshape(D, H, DV)[:, HEADS].reshape(D, H * DV)
    W1 = np.concatenate([tiles(wab, 1), tiles(A("Wk"), 3), tiles(A("Wq"), 3), tiles(hv(A("Wv")), 6),
                         tiles(hv(A("Wg")), 6)])
    cw = np.concatenate([A("conv_wk").reshape(3, 128, 4), A("conv_wq").reshape(3, 128, 4),
                         A("conv_wv").reshape(H, DV, 4)[HEADS]]).transpose(1, 0, 2)
    row = lambda a: np.broadcast_to(a[None, :], (128, H))
    gate, up = tiles(v["L0_ffn_w_gate"].T, 16), tiles(v["L0_ffn_w_up"].T, 16)
    down = v["L0_ffn_w_down"].T.reshape(16, 128, 1, D)
    arrays = {
        "x": v["L0_attn_hidden_states"],
        "W1": W1,
        "cw": cw,
        "dtb": row(A("dt_bias")[HEADS]),
        "alog": row(A("A_log")[HEADS]),
        "nw": A("norm_weight").reshape(128, 1),
        "Wo": A("Wo").reshape(H, DV, D)[HEADS].transpose(1, 0, 2),
        "cT": v["L0_c"].T.reshape(4, 128, 4).transpose(1, 0, 2),
        "wmod": v["L0_wmod"].reshape(4, 128, 6 * D).transpose(1, 0, 2),
        "wf": np.concatenate([gate.reshape(16, 128, 1, D), up.reshape(16, 128, 1, D), down], axis=2),
        "cst": constants(),
    }
    arrays = {k: np.ascontiguousarray(a) for k, a in arrays.items()}
    nc = bacc.Bacc("TRN2", target_bir_lowering=False, num_devices=1)
    h = {k: nc.dram_tensor("in_" + k, a.shape, mybir.dt.from_np(a.dtype), kind="ExternalInput").ap()
         for k, a in arrays.items()}
    out = nc.dram_tensor("out", (NB, SEQ, D), mybir.dt.float32, kind="ExternalOutput").ap()
    build(nc, h["x"], h["W1"], h["cw"], h["dtb"], h["alog"], h["nw"], h["Wo"], h["cT"], h["wmod"], h["wf"], h["cst"],
          out)
    r = run_bass_kernel_spmd(nc, [{"in_" + k: a for k, a in arrays.items()}], core_ids=[0])
    return r.results[0]["out"]
```

```python
import numpy as np
import concourse.bass as bass
from concourse import mybir

NB, SEQ, D, H, DK, DV, FF = 4, 512, 512, 6, 64, 128, 2048
NS = SEQ // 128
HEADS = [0, 2, 4, 1, 3, 5]
EPS = 1e-5
NT1 = 19
CONSTS = ["ident", "SG", "LE", "CH0", "CH1", "BO", "ON", "EP"]


def constants():
    i = np.arange(128)
    r, c = i[:, None], i[None, :]
    same = (r // 64) == (c // 64)
    m = {
        "ident": r == c,
        "SG": (r > c) & same,
        "LE": (r <= c) & same,
        "CH0": (r < 64) & (c >= 0),
        "CH1": (r >= 64) & (c >= 0),
        "BO": same,
        "ON": np.full((128, 128), 1.0 / 128),
        "EP": np.full((128, 128), EPS * DK),
    }
    cols = [m[n].astype(np.float32) for n in CONSTS]
    sel = np.zeros((128, NB * 128), np.float32)
    for b in range(NB):
        sel[b, b * 128:(b + 1) * 128] = 1.0
    extra = np.zeros((128, 8), np.float32)
    extra[:, 0] = EPS
    extra[:, 1] = 1.0
    return np.ascontiguousarray(np.concatenate(cols + [sel, extra], axis=1))


class Eng:

    def __init__(self, sem, serial=False):
        self.sem, self.n, self.q, self.seen, self.serial = sem, 0, [], {}, serial

    def wait(self, *toks):
        for t in toks:
            if t is None:
                continue
            if isinstance(t, (list, tuple)) and t and isinstance(t[0], (list, tuple)):
                self.wait(*t)
                continue
            if not t:
                continue
            sem, v = t
            if self.seen.get(id(sem), 0) < v:
                self.seen[id(sem)] = v
                self.q.append(lambda e, sem=sem, v=v: e.wait_ge(sem, v))

    def op(self, fn, *waits, inc=True):
        self.wait(*waits)
        if self.serial:
            self.wait((self.sem, self.n))
        if not inc:
            self.q.append(fn)
            return None
        self.n += 1
        self.q.append(lambda e: fn(e).then_inc(self.sem, 1))
        return (self.sem, self.n)

    def run(self, e):
        for f in self.q:
            f(e)


class Slot:

    def __init__(self, sem):
        self.sem, self.n = sem, 0

    def start(self, eng, out, in_, *waits):
        eng.wait(*waits)
        self.n += 16
        eng.q.append(lambda e: e.dma_start(out, in_).then_inc(self.sem, 16))
        return (self.sem, self.n)


class Ring:

    def __init__(self, n):
        self.n, self.i, self.free = n, -1, [[] for _ in range(n)]

    def take(self):
        self.i = (self.i + 1) % self.n
        return self.i, self.free[self.i]


def build(nc, x, W1, cw, dtb, alog, nw, Wo, cT, wmod, wg, cst, out):
    f32, f32r = mybir.dt.float32, mybir.dt.float32r
    ALU, ACT = mybir.AluOpType, mybir.ActivationFunctionType
    names = [0]

    def at(off, shape, dt=f32):
        names[0] += 1
        n = 4
        for s in shape[1:]:
            n *= s
        assert off % 32 == 0 and off + n <= 229216, (off, n)
        return nc.alloc_sbuf_tensor_at(f"t{names[0]}", shape, dt, offset=off)

    class Map:
        def __init__(self, base):
            self.p = base

        def new(self, shape, dt=f32):
            n = 4
            for s in shape[1:]:
                n *= s
            t = at(self.p, shape, dt)
            self.p += (n + 31) // 32 * 32
            return t

    scrU = nc.dram_tensor("scrU", (16, 128, 15, 128), f32).ap()
    scrA = nc.dram_tensor("scrA", (NS, 96, 32, 32), f32).ap()
    scrP = nc.dram_tensor("scrP", (NS, 96, 32, 32), f32).ap()
    scrX = nc.dram_tensor("scrX", (16, 128, D), f32).ap()

    M = Map(16384)
    NC_ = len(CONSTS) * 128
    cs = M.new([128, NC_ + 512 + 8])
    C = {n: cs[:, i * 128:(i + 1) * 128] for i, n in enumerate(CONSTS)}
    sel = cs[0:4, NC_:NC_ + 512]
    epsc, onec = cs[:, NC_ + 512:NC_ + 513], cs[:, NC_ + 513:NC_ + 514]
    ident = C["ident"]
    cwt = M.new([128, 12, 4])
    nwt = M.new([128, 1])
    dtbt, nexpA = M.new([128, H]), M.new([128, H])
    modT = M.new([128, 4, 4, NB])
    gnat = M.new([4, 2, D])
    g, nbeta, beta, nbg = (M.new([128, 16, H]) for _ in range(4))
    EX = M.new([128, NS, 4, 24])
    GC = M.new([128, NS, 2, NB, 3])
    mv, rs = M.new([128, 16, 2]), M.new([128, 16])
    st6 = M.new([128, 2, 6])
    kT = M.new([128, 3, NB * SEQ])
    P = M.new([128, NS, 24, 128])
    top = M.p
    A_ = Map(top)
    Hhi, Hlo = A_.new([128, 4, NB * SEQ], f32r), A_.new([128, 4, NB * SEQ], f32r)
    a_after_h = A_.p
    Wraw = [A_.new([128, 4, 128]) for _ in range(2)]
    Whi = [A_.new([128, 4, 128], f32r) for _ in range(2)]
    Wlo = [A_.new([128, 4, 128], f32r) for _ in range(2)]
    Y = [A_.new([128, SEQ]) for _ in range(2)]
    O = [A_.new([128, SEQ]) for _ in range(3)]
    Am = A_.new([128, NS, 24, 32])
    GMT = A_.new([128, H, 128])
    EV = A_.new([128, H, 128])
    Ab = [A_.new([128, H, 128]) for _ in range(2)]
    p3 = top - 24 * 128 * 4
    nAps, Pps = [A_.new([96, 32, 32]), at(p3, [96, 32, 32])], [A_.new([96, 32, 32]), at(p3 + 4096, [96, 32, 32])]
    tmps = [A_.new([96, 256]), at(p3 + 8192, [96, 256])]
    assert A_.p <= 229216, A_.p
    p_off = top - NS * 24 * 128 * 4
    S_ = Map(p_off)
    wm = [S_.new([128, 4, 512]) for _ in range(2)]
    modn = S_.new([4, 6, 512])
    X = [S_.new([128, D]) for _ in range(3)]
    XN = [S_.new([128, D]) for _ in range(2)]
    HF = [S_.new([128, 4, 128]) for _ in range(2)]
    cTt = S_.new([128, 4, 4])
    sgn = S_.new([4, 2, D])
    assert S_.p <= top
    w_off = a_after_h + 11 * 2048 + 24 * 512
    Wearly = [at(w_off + i * 2048, [128, 4, 128], f32r) for i in range(4)]
    WH, WL = Whi + Wearly[0:2], Wlo + Wearly[2:4]
    am_off = a_after_h + 11 * 2048
    ab = at(am_off, [12, NB * SEQ])
    zt = at(am_off + 8192, [128, 16, 12])
    z2 = at(am_off + 8192 + 768, [128, 16, H])
    z3 = at(am_off + 8192 + 768 + 384, [128, 16, H])
    B_ = Map(top)
    S = B_.new([128, NB * 3, 128])
    Sg = B_.new([128, 3, 128])
    U = [B_.new([128, 15, 128]) for _ in range(2)]
    GMb, Eb = B_.new([128, H, 128]), B_.new([128, H, 128])
    Kbg, Kd, Qg = B_.new([128, 3, 2, 64]), [B_.new([128, 3, 2, 64]) for _ in range(2)], B_.new([128, 3, 2, 64])
    Vb = [B_.new([128, H, 128]) for _ in range(2)]
    QgT, WT = [B_.new([128, 3, 128]) for _ in range(2)], [B_.new([128, 3, 128]) for _ in range(2)]
    PAn, PAT = B_.new([128, H, 128]), [B_.new([128, H, 128]) for _ in range(2)]
    dl = B_.new([128, H, 128])
    O2, Q2, R, OZ = B_.new([128, H, 128]), B_.new([128, 3, 128]), B_.new([128, H, 128]), B_.new([128, H, 128])
    XB = [B_.new([128, D]) for _ in range(2)]
    YB = [B_.new([128, D]) for _ in range(2)]
    Wot = B_.new([128, H, D])
    gaB = B_.new([128, NB, D])
    assert B_.p <= 229216, B_.p
    c0 = Map(p_off - 3 * NB * SEQ * 4)
    yacc = c0.new([128, 16, D])
    gbB = c0.new([128, NB, D])
    XC = [c0.new([128, D]) for _ in range(2)]
    XNC = [c0.new([128, D]) for _ in range(2)]
    hfc_off = c0.p
    HFC = [c0.new([128, 4, 128]) for _ in range(2)]
    XC += [at(hfc_off + i * 2048, [128, D]) for i in range(2)]
    SI = [c0.new([128, 512]) for _ in range(2)]
    XF = [at(c0.p + i * 2048, [128, D]) for i in range(4)]
    FH = [c0.new([128, 512], f32r) for _ in range(4)]
    FL = [c0.new([128, 512], f32r) for _ in range(4)]
    assert c0.p <= top, (c0.p, top)
    GF = at(a_after_h, [128, 512])
    C_ = Map(229216 - 9 * 6144)
    assert a_after_h + 2048 <= C_.p
    Gb = [C_.new([128, 3, 512], f32r) for _ in range(5)]
    assert C_.p >= B_.p, (C_.p, B_.p)
    Graw = C_.new([128, 3, 512])
    Gb += [C_.new([128, 3, 512], f32r) for _ in range(3)]
    Ghi, Glo = [Gb[5], Gb[7], Gb[0], Gb[2]], [Gb[6], Gb[4], Gb[1], Gb[3]]

    PSt = nc.alloc_psum_tensor("ps", [128, 8, 512], f32)

    def bank(i):
        return PSt[:, i, :]

    def pair(i):
        return PSt[:, 2 * i:2 * i + 2, 0:384].rearrange("p a (m t) -> p a m t", m=3)

    def heads(t):
        return t.rearrange("p (a m) t -> p a m t", a=2)

    nsem = [0]

    def sem():
        nsem[0] += 1
        return nc.alloc_semaphore(f"s{nsem[0]}")

    PE, V, SC, SY = (Eng(sem()) for _ in range(4))
    G = Eng(sem(), serial=True)

    def slots(n):
        return [Slot(sem()) for _ in range(n)]

    def bc(ap, axis, shape):
        return ap.unsqueeze(axis).broadcast_to(shape)

    def mm(o, l, r, start, stop, last=False, *waits):
        return PE.op(lambda e: e.matmul(o, l, r, start=start, stop=stop, skip_group_check=True), *waits, inc=last)

    def mm3(o, lh, ll, rh, rl, first, stop, last=False):
        mm(o, lh, rh, first, False)
        mm(o, ll, rh, False, False)
        return mm(o, lh, rl, False, stop, last)

    def tr(o, i, idn, last=False, *waits):
        return PE.op(lambda e: e.transpose(o, i, idn), *waits, inc=last)

    def act(o, i, f, *waits, **k):
        return SC.op(lambda e: e.activation(o, i, f, **k), *waits)

    def tt(E, o, a, b, op, *waits):
        return E.op(lambda e: e.tensor_tensor(o, a, b, op), *waits)

    def ts(E, o, a, s1, s2, o1, o2, *waits):
        if s2 is None:
            return E.op(lambda e: e.tensor_scalar(o, a, s1, None, o1), *waits)
        return E.op(lambda e: e.tensor_scalar(o, a, s1, s2, o1, o2), *waits)

    def stt(o, a, s, b, o1, o2, *waits):
        return V.op(lambda e: e.scalar_tensor_tensor(o, a, s, b, o1, o2), *waits)

    def cp(E, o, i, *waits):
        return E.op(lambda e: e.tensor_copy(o, i), *waits)

    SC.q.append(lambda e: e.preload_act_table_set("silu_and_others"))
    k_c, k_cw, k_nw, k_dt, k_al, k_cT, k_id = slots(7)
    x_slots = slots(3)
    x_ring = Ring(3)

    def load_x(u):
        s, b = u // 4, u % 4
        r, free = x_ring.take()
        return r, x_slots[r].start(SY, X[r][:, :], x[b, s * 128:(s + 1) * 128, :], free)

    order = [s * 4 + b for b in range(4) for s in range(4)]
    xl = [load_x(order[0]), load_x(order[1])]
    t_id = k_id.start(SY, cs[:, 0:128], cst[:, 0:128])
    t_ep = k_c.start(SY, cs[:, NC_ + 512:NC_ + 520], cst[:, NC_ + 512:NC_ + 520])
    t_cT = k_cT.start(SY, cTt[:, :, :], cT)
    wm_slots = slots(2)
    wm_ring = Ring(2)
    t_wm = []

    def load_mod(i):
        r, free = wm_ring.take()
        t_wm.append((r, wm_slots[r].start(SY, wm[r][:, :, :], wmod[:, :, i * 512:(i + 1) * 512], free)))

    load_mod(0)
    load_mod(1)
    t_cst = Slot(sem()).start(SY, cs[:, 128:NC_ + 512], cst[:, 128:NC_ + 512])
    xl.append(load_x(order[2]))
    t_cw = k_cw.start(SY, cwt[:, :, :], cw)
    t_nw = k_nw.start(SY, nwt[:, :], nw)
    t_dt = k_dt.start(SY, dtbt[:, :], dtb)
    t_al = k_al.start(SY, nexpA[:, :], alog)

    tiles = [0, 9, 1, 10, 2, 11, 3, 12, 4, 13, 5, 14, 6, 7, 8]
    WSEQ = [0, 1, 2, 3] + [4 + n for n in tiles]
    w_slots = slots(2)
    w_ring = Ring(2)
    wh_ring = Ring(4)

    def load_w(j):
        r, free = w_ring.take()
        return r, w_slots[r].start(SY, Wraw[r][:, :, :], W1[WSEQ[j]], free)

    t_silu = act(cTt[:, :, :], cTt[:, :, :], ACT.Silu, t_cT)
    SC.q.append(lambda e: e.preload_act_table_set("natural_log_exp_and_others"))
    t_nexp0 = act(nexpA[:, :], nexpA[:, :], ACT.Exp, t_al)
    t_nexp = ts(V, nexpA[:, :], nexpA[:, :], -1.0, None, ALU.mult, None, t_nexp0)

    bfree = [[] for _ in range(8)]

    def split_w(j, ld):
        r, t = ld
        h, free = wh_ring.take()
        a = act(WH[h][:, :, :], Wraw[r][:, :, :], ACT.Copy, t, free)
        b = tt(V, WL[h][:, :, :], Wraw[r][:, :, :], WH[h][:, :, :].bitcast(f32), ALU.subtract, a, free)
        w_ring.free[r] = [b]
        return h, b

    def mod_rows(i):
        r, t = t_wm[i]
        bk = 6 + i % 2
        PE.wait(t, t_silu, bfree[bk])
        for k in range(4):
            tk = mm(bank(bk)[0:4, :], cTt[:, k, :], wm[r][:, k, :], k == 0, k == 3, k == 3)
        wm_ring.free[r] = [tk]
        if i in (1, 4):
            tm = ts(V, modn[:, i, :], bank(bk)[0:4, :], 1.0, None, ALU.add, None, tk)
        else:
            tm = cp(V, modn[:, i, :], bank(bk)[0:4, :], tk)
        bfree[bk] = [tm]
        return tm

    def mod_cols(i, dst, tm):
        PE.wait(tm, t_id, bfree[6])
        for k in range(4):
            tk = tr(bank(6)[:, k * 4:k * 4 + 4], modn[:, i, k * 128:(k + 1) * 128], ident[0:4, 0:4], k == 3)
        t = cp(V, modT[:, dst, :, :].rearrange("p k b -> p (k b)"), bank(6)[:, 0:16], tk)
        bfree[6] = [t]
        return t


    hf_free = [[], []]
    xn_free = [[], []]
    st_free = [[], []]

    def rstd(u, src, t_src):
        n = u % 2
        a = V.op(lambda e: e.bn_stats(st6[:, n, :], src), t_src, st_free[n])
        a = V.op(lambda e: e.bn_aggr(mv[:, u, :], st6[:, n, :]), a)
        st_free[n] = [a]
        l = act(rs[:, u:u + 1], mv[:, u, 1:2], ACT.Ln, a, bias=epsc)
        return act(rs[:, u:u + 1], rs[:, u:u + 1], ACT.Exp, l, scale=-0.5)

    def norms(us, src, stats, XNs, HFs, i_sh, i_sc, t_mod, ring, base, res):
        N, st = len(us), {}
        for n in range(N + 4):
            if n >= 4:
                u, o = us[n - 4], st[n - 4]
                c = (u % 4) * SEQ + (u // 4) * 128
                lo = tt(G, Hlo[:, :, c:c + 128], HFs[o["m"]][:, :, :], Hhi[:, :, c:c + 128].bitcast(f32),
                        ALU.subtract, o["hi"])
                hf_free[o["m"]] = [lo]
                res[u] = lo
            if n >= 3 and n - 3 < N:
                u, o = us[n - 3], st[n - 3]
                b, m = u % 4, n % 2
                c = b * SEQ + (u // 4) * 128
                hs = []
                for k in range(4):
                    i_, o_ = bank(o["bk"])[:, k * 128:(k + 1) * 128], HFs[m][:, k, :]
                    s1, s2 = modT[:, i_sc, k, b:b + 1], modT[:, i_sh, k, b:b + 1]
                    if n % 2:
                        hs.append(ts(V, o_, i_, s1, s2, ALU.mult, ALU.add, o["tk"], t_mod, hf_free[m]))
                    else:
                        hs.append(act(o_, i_, ACT.Identity, o["tk"], t_mod, hf_free[m], scale=s1, bias=s2))
                ring.free[o["r"]] = [hs[3]]
                o["hi"] = act(Hhi[:, :, c:c + 128], HFs[m][:, :, :], ACT.Copy, hs[3])
                o["m"] = m
            if n >= 2 and n - 2 < N:
                o = st[n - 2]
                m = n % 2
                o["r"], free = ring.take()
                o["bk"] = base + o["r"]
                PE.wait(o["xn"], free, t_id)
                for k in range(4):
                    tk = tr(bank(o["bk"])[:, k * 128:(k + 1) * 128], XNs[m][:, k * 128:(k + 1) * 128], ident, k == 3)
                xn_free[m] = [tk]
                o["tk"] = tk
            if n >= 1 and n - 1 < N:
                u, o = us[n - 1], st[n - 1]
                m = (n + 1) % 2
                o["xn"] = ts(V, XNs[m][:, :], o["x"], mv[:, u, 0:1], rs[:, u:u + 1], ALU.subtract, ALU.mult, o["l"],
                             xn_free[m])
                o["rd"].append(o["xn"])
            if n < N:
                xt, t, rd = src(n)
                st[n] = {"x": xt, "l": rstd(us[n], xt, [t, t_ep]) if stats else t, "rd": rd}
            yield

    wl = [load_w(0), load_w(1)]

    def src_x(n):
        r, t = xl[n]
        rd = []
        x_ring.free[r] = rd
        return X[r][:, :], t, rd

    t_hn = {}
    n_ring = Ring(2)
    t_m = []

    def norm_x():
        for n, _ in enumerate(norms(order, src_x, True, XN, HF, 0, 1, t_m, n_ring, 4, t_hn)):
            if 3 <= n + 2 < 16:
                xl.append(load_x(order[n + 2]))
            yield

    nrm = norm_x()
    next(nrm)
    next(nrm)
    m0, m1 = mod_rows(0), mod_rows(1)
    t_m += [mod_cols(0, 0, m0), mod_cols(1, 1, m1)]
    for _ in range(6):
        next(nrm)
    load_mod(2)
    load_mod(3)

    def late_mods(early):
        tms = early + [mod_rows(4), mod_rows(5)]
        t_sb, t_cb = mod_cols(3, 2, tms[1]), mod_cols(4, 3, tms[2])
        for n, i in ((0, 2), (1, 5)):
            src = modn[:, i, :]
            a = stt(gnat[:, n, :], src, -1.0, src, ALU.mult, ALU.max, tms[i - 2])
            a = ts(V, gnat[:, n, :], gnat[:, n, :], 0.25, None, ALU.max, None, a)
            c_ = ts(V, sgn[:, n, :], src, 0.0, 2.0, ALU.is_ge, ALU.mult, a)
            c_ = ts(V, sgn[:, n, :], sgn[:, n, :], -1.0, None, ALU.add, None, c_)
            t = tt(V, gnat[:, n, :], gnat[:, n, :], sgn[:, n, :], ALU.mult, c_)
        return t_sb, t_cb, t

    pr = Ring(4)

    def project(h, tw, b):
        i, free = pr.take()
        PE.wait(free, tw, t_hn[12 + b])
        c = slice(b * SEQ, (b + 1) * SEQ)
        for k in range(4):
            t = mm3(bank(i), WH[h][:, k, :], WL[h][:, k, :], Hhi[:, k, c], Hlo[:, k, c], k == 0, k == 3, k == 3)
        return i, t

    y_ring, o_ring = Ring(2), Ring(3)
    o_slots = slots(3)

    def conv(i, t, j, dst=None, between=lambda: None):
        y, free = y_ring.take() if dst is None else (None, [])
        p, yy = bank(i), Y[y] if dst is None else dst
        w = lambda n: cwt[:, j, n:n + 1]
        a = act(yy[:, :], p, ACT.Copy, t, free, t_cw, scale=w(3))
        for n in (2, 1, 0):
            d = 3 - n
            a = stt(yy[:, d:SEQ], p[:, 0:SEQ - d], w(n), yy[:, d:SEQ], ALU.mult, ALU.add, a)
            between()
        pr.free[i] = [a]
        return y, a

    t_scrU = {}

    def store_unit(o, t, tile, b):
        dst = scrU.rearrange("(s b) p j t -> b j p s t", b=4)[b, tile]
        src = O[o][:, :].rearrange("p (s t) -> p s t", s=4)
        tk = o_slots[o].start(SY, dst, src, t)
        o_ring.free[o] = [tk]
        t_scrU[(tile, b)] = tk

    def next_w(j):
        got_w = split_w(j, wl[j])
        if j + 2 < NT1:
            wl.append(load_w(j + 2))
        return got_w

    hw = [next_w(j) for j in range(4)]
    t_k = {}
    for b in range(4):
        for m in range(4):
            h, tw = hw[m]
            i, t = project(h, tw, b)
            if m == 0:
                t_ab = cp(V, ab[:, b * SEQ:(b + 1) * SEQ], bank(i)[0:12, :], t)
                pr.free[i] = [t_ab]
            else:
                _, t_k[(m - 1, b)] = conv(i, t, m - 1, kT[:, m - 1, b * SEQ:(b + 1) * SEQ])
            next(nrm, None)
        if b == 1:
            early = [mod_rows(2), mod_rows(3)]
            load_mod(4)
            load_mod(5)
    wh_ring = Ring(2)
    wh_ring.free = [[t], [t]]
    SQ = [at(w_off, [128, 3, SEQ]), at(w_off + 6144, [128, 3, SEQ])]
    sq_free = [[t], [t]]
    SC.q.append(lambda e: e.preload_act_table_set("silu_and_others"))
    PE.wait(t_ab, t_id, t_cst, bfree[7])
    for u in range(16):
        s, b = u // 4, u % 4
        tk = tr(bank(7)[:, u * 12:u * 12 + 12], ab[:, b * SEQ + s * 128:b * SEQ + s * 128 + 128],
                ident[0:12, 0:12], u == 15)
    t_z = cp(V, zt[:, :, :].rearrange("p u c -> p (u c)"), bank(7)[:, 0:192], tk)
    bfree[7] = [t_z]
    SC.q.append(lambda e: e.preload_act_table_set("natural_log_exp_and_others"))
    sh = [128, 16, H]
    t_a = tt(V, zt[:, :, 0:6], zt[:, :, 0:6], bc(dtbt[:, :], 1, sh), ALU.add, t_z, t_dt)
    a = act(z2[:, :, :], zt[:, :, 0:6], ACT.Abs, t_a)
    a = act(z2[:, :, :], z2[:, :, :], ACT.Exp, a, scale=-1.0)
    a = act(z2[:, :, :], z2[:, :, :], ACT.Ln, a, bias=onec)
    a = stt(z3[:, :, :], zt[:, :, 0:6], 0.0, z2[:, :, :], ALU.max, ALU.add, a)
    t_g = tt(V, g[:, :, :], z3[:, :, :], bc(nexpA[:, :], 1, sh), ALU.mult, a, t_nexp)
    a = act(z2[:, :, :], zt[:, :, 6:12], ACT.Exp, a, scale=-1.0)
    a = ts(V, z2[:, :, :], z2[:, :, :], 1.0, None, ALU.add, None, a)
    t_be = V.op(lambda e: e.reciprocal(beta[:, :, :], z2[:, :, :]), a)
    t_nb = ts(V, nbeta[:, :, :], beta[:, :, :], -1.0, None, ALU.mult, None, t_be)
    t_kb, t_sq = {}, {}
    mods = {}
    setup_done = [list(t_hn.values()), xn_free, hf_free]

    def k_square(b):
        kk = kT[:, :, b * SEQ:(b + 1) * SEQ]
        a = act(kk, kk, ACT.Silu, [t_k[(m, b)] for m in range(3)])
        t_sq[b] = tt(G, SQ[b % 2][:, :, :], kk, kk, ALU.mult, a, sq_free[b % 2])

    def k_norm():
        k_square(0)
        yield
        for b in range(4):
            y = SQ[b % 2]
            kk = kT[:, :, b * SEQ:(b + 1) * SEQ]
            PE.wait(t_sq[b], t_cst, pairs.free)
            for m in range(3):
                t = mm(bank(4 + m), C["BO"], y[:, m, :], True, True, m == 2)
            SC.q.append(lambda e: e.preload_act_table_set("natural_log_exp_and_others"))
            a = act(y[:, :, :], PSt[:, 4:7, :], ACT.Ln, t)
            pairs.free = [[a], [a]]
            a = act(y[:, :, :], y[:, :, :], ACT.Exp, a, scale=-0.5)
            SC.q.append(lambda e: e.preload_act_table_set("silu_and_others"))
            t_kb[b] = tt(V, kk, kk, y[:, :, :], ALU.mult, a)
            sq_free[b % 2] = [t_kb[b]]
            if b < 3:
                k_square(b + 1)
            if b == 1:
                bfree[:] = [[a]] * 8
                mods["sb"], mods["cb"], mods["gn"] = late_mods(early)
                setup_done.append(list(mods.values()))
                pairs.free = [pairs.free[0], [a] + bfree[6] + bfree[7]]
            yield


    pairs = Ring(2)
    pairs.free = [[bfree[4], bfree[5], n_ring.free], [bfree[6], bfree[7]]]

    def pfree(i, t):
        pairs.free[i] = [t]

    ab_ring = Ring(2)
    a_slots = [slots(4), slots(4)]
    for q in (0, 64):
        t_am0 = G.op(lambda e, q=q: e.memset(Am[q:q + 32, :, :, :], 0.0), t_g, t_nb, t_z)
    t_am = {}
    t_ex, a_out, t_pz, din, t_P = {}, {}, {}, {}, {}
    gms = [GMT, EV, Ab[0], Ab[1]]
    gm_free, ev_free = [], []

    def decay_mult(u, GMx, free_gm):
        return tt(V, GMx[:, :, :], bc(C["SG"], 1, [128, H, 128]), bc(g[:, u, :], 2, [128, H, 128]), ALU.mult,
                  t_g, t_cst, free_gm)

    def decay_exp(a, GMx, Ex, free_e):
        p, free = pairs.take()
        PE.wait(a, free)
        for par in range(2):
            t = mm(PSt[:, 4 + 2 * p + par, 0:384], C["LE"], GMx[:, 3 * par:3 * par + 3, :], True, True, par == 1)
        e = act(heads(Ex), pair(2 + p), ACT.Exp, t, free_e)
        pfree(p, e)
        return t, e

    def sums(s):
        p, free = pairs.take()
        bk = bank(4 + 2 * p)
        rhs = g[:, 4 * s:4 * s + 4, :].rearrange("p u h -> p (u h)")
        PE.wait(free, t_g, t_cst)
        for n, w in enumerate(("LE", "SG", "CH0", "CH1")):
            t = mm(bk[:, n * 24:n * 24 + 24], C[w], rhs, n == 0, True, n == 3)
        e = act(EX[:, s, :, :].rearrange("p n h -> p (n h)"), bk[:, 0:96], ACT.Exp, t)
        pfree(p, e)
        v = EX[:, s, :, :].rearrange("p n (b a m) -> p n b a m", b=4, a=2)
        for par in range(2):
            q = slice(64 * par, 64 * par + 64)
            for c in range(2):
                a = cp(V, GC[q, s, c, :, :], v[q, 2 + c, :, par, :], e)
        w = tt(V, nbg[:, 4 * s:4 * s + 4, :].rearrange("p u h -> p (u h)"),
               nbeta[:, 4 * s:4 * s + 4, :].rearrange("p u h -> p (u h)"), EX[:, s, 0, :], ALU.mult, e, t_nb)
        t_ex[s] = w

    def inverse_1(s):
        nonlocal gm_free, ev_free
        e_free = setup_done if s < 3 else pp_free[1]
        if s == 0:
            gm_free, ev_free = [t_kb[3], t_kb[2]], [t_kb[3], t_kb[2]]
            ab_ring.free = [gm_free, gm_free]
        gf = [gm_free, ev_free, ab_ring.free[0], ab_ring.free[1]]
        gm = [decay_mult(s * 4 + b, gms[b], gf[b]) for b in range(4)]
        yield
        SC.q.append(lambda e: e.preload_act_table_set("natural_log_exp_and_others"))
        E = []
        for b in range(4):
            t, e = decay_exp(gm[b], gms[b], P[:, s, b * 6:b * 6 + 6, :], e_free)
            E.append(e)
        gm_free, ev_free = [t], [t]
        ab_ring.free = [[t], [t]]
        sums(s)
        SC.q.append(lambda e: e.preload_act_table_set("silu_and_others"))
        yield
        toks, am = [], []
        for b in range(4):
            u = s * 4 + b
            p, free = pairs.take()
            PE.wait(free, t_kb[b])
            for m in range(3):
                for par in range(2):
                    r = slice(64 * par, 64 * par + 64)
                    kk = kT[r, m, b * SEQ + s * 128:b * SEQ + s * 128 + 128]
                    t = mm(PSt[:, 4 + 2 * p + par, m * 128:m * 128 + 128], kk, kk, True, True, m == 2 and par == 1)
            i, free = ab_ring.take()
            ev = a = tt(V, heads(Ab[i][:, :, :]), pair(2 + p), heads(P[:, s, b * 6:b * 6 + 6, :]), ALU.mult, t, E[b],
                        free)
            pfree(p, a)
            a = tt(G, Ab[i][:, :, :], Ab[i][:, :, :], bc(nbeta[:, u, :], 2, [128, H, 128]), ALU.mult, a, t_nb)
            for c in range(2):
                q = slice(64 * c + 32, 64 * c + 64)
                t = cp(G, Am[q, s, b * 6:b * 6 + 6, :], Ab[i][q, :, 64 * c:64 * c + 32], a, t_am0)
            am.append(t)
            d = []
            for k in range(4):
                q = slice(32 * k, 32 * k + 32)
                d.append(a_slots[i][k].start(SY, scrA[s, k * 24 + b * 6:k * 24 + b * 6 + 6].rearrange("h t i -> t h i"),
                                             Ab[i][q, :, q], a))
            ab_ring.free[i] = [am[-1]] + d
            toks += d
            if b == 3:
                a_out[s], t_am[s] = toks, am
                t_pz[s] = G.op(lambda e: e.memset(P[:, s, :, :], 0.0), ev)
            yield

    nap_slots, pp_slots = slots(2), slots(2)
    pin_slots = slots(4)
    pp_free = [[], setup_done]

    def inverse_2(s, E, x):
        nAp, Pp, tmp = nAps[x], Pps[x], tmps[x]
        t = nap_slots[x].start(SY, nAp[:, :, :], scrA[s], a_out[s], pp_free[x])
        a = G.op(lambda e: e.memset(Pp[:, :, :], 0.0), pp_free[x])
        dg = Pp[:, :, :].rearrange("p a b -> p (a b)")[:, 0:1024:33]
        a = G.op(lambda e: e.memset(dg, 1.0), a)
        yield
        E.wait(t)
        for j in range(31):
            n, w = j + 1, 31 - j
            tm = tmp[:, 0:n * w].rearrange("p (c t) -> p c t", c=n)
            a = tt(E, tm, Pp[:, 0:n, j:j + 1].broadcast_to([96, n, w]),
                   bc(nAp[:, j + 1:32, j], 1, [96, n, w]), ALU.mult, a)
            yield
            a = tt(E, Pp[:, 0:n, j + 1:32], Pp[:, 0:n, j + 1:32], tm, ALU.add, a)
            yield
        o = pp_slots[x].start(SY, scrP[s], Pp[:, :, :], a)
        pp_free[x] = [a, o]
        din[s] = []
        for k in range(4):
            q = slice(32 * k, 32 * k + 32)
            din[s].append(pin_slots[k].start(SY, P[q, s, :, q],
                                             scrP[s, k * 24:k * 24 + 24].rearrange("h c t -> c h t"), o, t_pz[s]))

    def merge(s):
        nonlocal gm_free, ev_free
        t_e0 = G.op(lambda e: e.memset(EV[:, :, :], 0.0), ev_free)
        ev_free = [t_e0]
        for b in range(5):
            if b:
                hb = slice(b * 6 - 6, b * 6)
                p, free = pairs.take()
                PE.wait(free, v, tT)
                for h_ in range(6):
                    t2 = mm(PSt[:, 4 + 2 * p + h_ // 3, (h_ % 3) * 64:(h_ % 3) * 64 + 64], GMT[:, h_, :],
                            EV[:, h_, :].rearrange("p (c t) -> p c t", c=2)[:, :, 32:64], True, True, h_ == 5)
                gm_free, ev_free = [t2], [t2]
                for c in range(2):
                    q, w = slice(64 * c, 64 * c + 32), slice(64 * c + 32, 64 * c + 64)
                    src = PSt[q, 4 + 2 * p:6 + 2 * p, 0:192].rearrange("p a (m c t) -> p a m c t", m=3, c=2)[:, :, :, c, :]
                    a = cp(V, heads(P[:, s, hb, :])[q, :, :, w], src, t2, tT)
                pfree(p, a)
                t_P[(s, b - 1)] = a
            if b < 4:
                hb = slice(b * 6, b * 6 + 6)
                tT = V.op(lambda e, hb=hb: e.transpose(GMT[:, :, :], P[:, s, hb, :]), din[s], t_pz[s], gm_free)
                p, free = pairs.take()
                PE.wait(free, din[s], t_pz[s], t_am[s][b])
                for c in range(2):
                    for h_ in range(6):
                        t = mm(PSt[64 * c:64 * c + 32, 4 + 2 * p + c, h_ * 32:h_ * 32 + 32],
                               Am[:, s, b * 6 + h_, :], P[:, s, b * 6 + h_, 64 * c + 32:64 * c + 64], True, True,
                               h_ == 5)
                for c in range(2):
                    q, w = slice(64 * c, 64 * c + 32), slice(64 * c + 32, 64 * c + 64)
                    v = act(EV[q, :, w], PSt[q, 4 + 2 * p + c, 0:192].rearrange("p (h t) -> p h t", h=6), ACT.Copy, t,
                            ev_free)
                pfree(p, v)
            yield

    lanes = [[(0, 1, k_norm()), (5, 1, inverse_1(0)), (11, 1, inverse_1(1)), (17, 1, inverse_1(2)), (26, 1, merge(0)),
              (35, 1, inverse_1(3)), (41, 1, merge(1)), (46, 1, merge(2)), (55, 1, merge(3))],
             [(12, 6, inverse_2(0, V, 0)), (24, 6, inverse_2(2, V, 0)), (41, 6, inverse_2(3, V, 0))],
             [(17, 4, inverse_2(1, G, 1))]]
    running = [None] * 3
    left = [0] * 3

    def begin(slot):
        for l, lane in enumerate(lanes):
            if running[l] is None and lane and lane[0][0] <= slot:
                running[l] = lane.pop(0)
            left[l] = running[l][1] if running[l] else 0

    def side(l, n=99):
        while running[l] and left[l] and n:
            left[l] -= 1
            n -= 1
            if next(running[l][2], "end") == "end":
                running[l] = None
                if lanes[l] and lanes[l][0][0] <= slot:
                    running[l] = lanes[l].pop(0)
                    left[l] += 1

    slot = 0
    SC.q.append(lambda e: e.preload_act_table_set("silu_and_others"))
    nxt = next_w(4)
    for n, tile in enumerate(tiles):
        h, tw = nxt
        for b in range(4):
            if b == 1 and n < 14:
                nxt = next_w(5 + n)
            begin(slot)
            i, t = project(h, tw, b)
            o, free = o_ring.take()
            if tile >= 9:
                a = act(O[o][:, :], bank(i), ACT.Silu, t, free)
                pr.free[i] = [a]
            else:
                y, a = conv(i, t, 3 + tile, between=lambda: side(1, 1))
                a = act(O[o][:, :], Y[y][:, :], ACT.Silu, a, free)
                y_ring.free[y] = [a]
            store_unit(o, a, tile, b)
            if b == 3:
                wh_ring.free[h] = [t]
            side(0)
            side(1)
            side(2)
            slot += 1
    while any(running) or any(lanes):
        begin(99)
        for l in range(3):
            side(l)
    t_sb, t_cb, t_gn = mods["sb"], mods["cb"], mods["gn"]
    SC.q.append(lambda e: e.preload_act_table_set("natural_log_exp_and_others"))

    p_ready = [t_P[(3, 3)], (V.sem, V.n), (PE.sem, PE.n), (SC.sem, SC.n), (G.sem, G.n)]
    stores = [t_scrU[k] for k in t_scrU]
    allA = p_ready + [o_ring.free]
    t_wo = slots(1)[0].start(SY, Wot[:, :, :], Wo, allA, stores)
    u_slots, u_ring = slots(2), Ring(2)
    xb_slots, xb_ring = slots(2), Ring(2)
    PE.wait(allA)
    V.wait(allA)
    SC.wait(allA)
    G.wait(allA)
    t_s0 = V.op(lambda e: e.memset(S[:, :, :], 0.0))
    t_d0 = V.op(lambda e: e.memset(dl[:, :, :], 0.0))

    def gate_rows(n, dst):
        for b in range(NB):
            p, free = pairs.take()
            bk = bank(4 + 2 * p)
            t = mm(bk, sel[:, b * 128:(b + 1) * 128], gnat[:, n, :], True, True, True, free, t_gn)
            a = act(dst[:, b, :], bk, ACT.Copy, t)
            pfree(p, a)
        return a

    t_ga = gate_rows(0, gaB)
    t_wo = act(Wot[:, :, :], Wot[:, :, :], ACT.Copy, t_wo, t_nw, scale=nwt[:, 0:1])

    gmb_free, eb_free, kbg_free, qg_free, pan_free = [], [], [], [], []
    r2 = {n: Ring(2) for n in ("Kd", "Vb", "QgT", "WT", "PAT")}
    dfree, ofree = [bfree[0], bfree[1], pr.free[0], pr.free[1]], [bfree[2], bfree[3], pr.free[2], pr.free[3]]
    t_S, S_read = {}, {}
    for b in range(4):
        t_S[b] = t_s0

    def load_u(u):
        r, free = u_ring.take()
        return r, u_slots[r].start(SY, U[r][:, :, :], scrU[u], allA, stores, free)

    ul = [load_u(0), load_u(1)]
    got = {}

    def prep(u):
        nonlocal gmb_free, eb_free, kbg_free, qg_free, pan_free
        s, b = u // 4, u % 4
        r, t_u = ul[u]
        col = slice(b * SEQ + s * 128, b * SEQ + s * 128 + 128)
        sc_ = lambda ap: bc(ap.rearrange("p (a m) -> p m a", a=2), 3, [128, 3, 2, 64])
        ex = lambda n: EX[:, s, n, b * 6:b * 6 + 6]
        q3 = lambda bk: bk[:, 0:384].rearrange("p (m a t) -> p m a t", m=3, a=2)
        o = {"r": r, "t_u": t_u}
        p, free = pairs.take()
        PE.wait(free, t_u)
        for m in range(3):
            tr(bank(4 + 2 * p)[:, m * 128:m * 128 + 128], kT[:, m, col], ident)
        for m in range(3):
            t = tr(bank(5 + 2 * p)[:, m * 128:m * 128 + 128], U[r][:, m, :], ident, m == 2)
        n_, free = r2["Kd"].take()
        o["Kd"] = n_
        o["t_kbg"] = tt(V, Kbg[:, :, :, :], q3(bank(4 + 2 * p)), sc_(nbg[:, u, :]), ALU.mult, t, kbg_free)
        o["t_kd"] = tt(V, Kd[n_][:, :, :, :], q3(bank(4 + 2 * p)), sc_(ex(1)), ALU.mult, free)
        t_qg = tt(V, Qg[:, :, :, :], q3(bank(5 + 2 * p)), sc_(ex(0)), ALU.mult, qg_free)
        pfree(p, t_qg)
        yield
        p, free = pairs.take()
        PE.wait(free)
        for h_ in range(6):
            t = tr(PSt[:, 4 + 2 * p + h_ // 3, (h_ % 3) * 128:(h_ % 3) * 128 + 128], U[r][:, 3 + h_, :], ident, h_ == 5)
        n_, free = r2["Vb"].take()
        o["Vb"] = n_
        o["t_vb"] = tt(V, heads(Vb[n_][:, :, :]), pair(2 + p),
                       bc(beta[:, u, :].rearrange("p (a m) -> p a m", a=2), 3, [128, 2, 3, 128]), ALU.mult, t, free)
        pfree(p, o["t_vb"])
        yield
        gm, e = decay_exp(decay_mult(u, GMb, gmb_free), GMb, Eb[:, :, :], eb_free)
        gmb_free = [gm]
        yield
        p, free = pairs.take()
        PE.wait(free, t_qg, o["t_kbg"], t_P[(s, b)])
        for m in range(3):
            t1 = tr(bank(4 + 2 * p)[:, m * 128:m * 128 + 128], Qg[:, m, :, :].rearrange("p a t -> p (a t)"), ident)
        for m in range(3):
            for par in range(2):
                t = mm(PSt[64 * par:64 * par + 64, 5 + 2 * p, m * 128:m * 128 + 128], Kbg[:, m, par, :],
                       P[:, s, b * 6 + par * 3 + m, :], True, True, m == 2 and par == 1)
        kbg_free, qg_free = [t], [t]
        n_, free = r2["QgT"].take()
        o["QgT"] = n_
        act(QgT[n_][:, :, :].rearrange("p m t -> p (m t)"), bank(4 + 2 * p)[:, 0:384], ACT.Copy, t, free)
        n_, free = r2["WT"].take()
        o["WT"] = n_
        o["t_wt"] = act(WT[n_][:, :, :].rearrange("p m t -> p (m t)"), bank(5 + 2 * p)[:, 0:384], ACT.Copy, free)
        pfree(p, o["t_wt"])
        yield
        p, free = pairs.take()
        PE.wait(free)
        for m in range(3):
            for par in range(2):
                q = slice(64 * par, 64 * par + 64)
                t = mm(PSt[:, 4 + 2 * p + par, m * 128:m * 128 + 128], U[r][q, m, :], kT[q, m, col], True, True,
                       m == 2 and par == 1)
        a = tt(V, heads(PAn[:, :, :]), pair(2 + p), heads(Eb[:, :, :]), ALU.mult, t, e, pan_free)
        pfree(p, a)
        eb_free = [a]
        p, free = pairs.take()
        PE.wait(free, a)
        for h_ in range(6):
            t = tr(PSt[:, 4 + 2 * p + h_ // 3, (h_ % 3) * 128:(h_ % 3) * 128 + 128], PAn[:, h_, :], ident, h_ == 5)
        pan_free = [t]
        n_, free = r2["PAT"].take()
        o["PAT"] = n_
        le = C["LE"].unsqueeze(1).unsqueeze(1).broadcast_to([128, 2, 3, 128])
        o["t_pat"] = tt(V, heads(PAT[n_][:, :, :]), pair(2 + p), le, ALU.mult, t, free)
        pfree(p, o["t_pat"])
        got[u] = o
        yield

    dl_w = [[t_d0], [t_d0]]
    dl_r = [[], []]
    sg_free = []

    def rec(u):
        nonlocal dfree, ofree, sg_free
        s, b = u // 4, u % 4
        o = got[u]
        kd, vb, qg, wt, pa = Kd[o["Kd"]], Vb[o["Vb"]], QgT[o["QgT"]], WT[o["WT"]], PAT[o["PAT"]]
        PE.wait(dfree, o["t_vb"], t_P[(s, b)], o["t_wt"])
        for m in range(3):
            for par in range(2):
                h_ = par * 3 + m
                mm(PSt[:, par, m * 128:m * 128 + 128], P[:, s, b * 6 + h_, :], vb[:, h_, :], m == 0, True)
        for c in range(2):
            q = slice(64 * c, 64 * c + 64)
            PE.wait(t_S[b])
            for m in range(3):
                for par in range(2):
                    w = slice(64 * par, 64 * par + 64)
                    t = mm(PSt[q, par, m * 128:m * 128 + 128], wt[w, m, q], S[w, b * 3 + m, :], False, True,
                           m == 2 and par == 1)
            t_dl = act(heads(dl[:, :, :])[q], pair(0)[q], ACT.Copy, t, dl_w[c], dl_r[0], dl_r[1])
            gcv = GC[:, s, c, b, :]
            t_sg = tt(G, Sg[:, :, :], S[:, b * 3:b * 3 + 3, :], bc(gcv, 2, [128, 3, 128]), ALU.mult, t_S[b], sg_free,
                      t_ex[s])
            if c == 0:
                PE.wait(ofree)
            for m in range(3):
                for par in range(2):
                    w = slice(64 * par, 64 * par + 64)
                    t_o1 = mm(PSt[:, 2 + par, m * 128 + 64 * c:m * 128 + 64 * c + 64], S[w, b * 3 + m, :],
                              qg[w, m, q], c == 0 and m == 0, True, m == 2 and par == 1)
            yield
            p, free = pairs.take()
            PE.wait(free, t_dl, o["t_kd"], o["t_pat"])
            for m in range(3):
                for par in range(2):
                    w = slice(64 * par, 64 * par + 64)
                    t_s = mm(PSt[w, 4 + 2 * p, m * 128:m * 128 + 128], kd[q, m, par, :], dl[q, par * 3 + m, :],
                             True, True, m == 2 and par == 1)
            a = tt(V, S[:, b * 3:b * 3 + 3, :], Sg[:, :, :],
                   bank(4 + 2 * p)[:, 0:384].rearrange("p (m t) -> p m t", m=3), ALU.add, t_s, t_sg, t_o1)
            t_S[b] = a
            sg_free = [a]
            pfree(p, a)
            for m in range(3):
                for par in range(2):
                    h_ = par * 3 + m
                    t_o = mm(PSt[:, 2 + par, m * 128 + 64 * c:m * 128 + 64 * c + 64], dl[:, h_, :], pa[:, h_, q],
                             False, True, m == 2 and par == 1)
            dl_r[c] = [t_o]
            yield
        dfree = [t_dl]
        o["t_o"] = t_o
        r2["Kd"].free[o["Kd"]] = [t_o]
        r2["Vb"].free[o["Vb"]] = [t_o]
        r2["QgT"].free[o["QgT"]] = [t_o]
        r2["WT"].free[o["WT"]] = [t_o]
        r2["PAT"].free[o["PAT"]] = [t_o]

    o2_free, q2_free, oz_free = [], [], []
    rr_free = []
    x1_slots, x1_ring = slots(2), Ring(2)
    xbl = {}

    def load_xb(u):
        s, b = u // 4, u % 4
        r, free = xb_ring.take()
        xbl[u] = (r, xb_slots[r].start(SY, XB[r][:, :], x[b, s * 128:(s + 1) * 128, :], allA, free))

    load_xb(0)
    load_xb(1)
    t_x1 = {}
    ho = lambda t: t[:, :, :].rearrange("p (a m) t -> p a (m t)", a=2)

    def post(u):
        nonlocal ofree, o2_free, q2_free, oz_free, rr_free
        s, b = u // 4, u % 4
        o = got[u]
        r = o["r"]
        op = PSt[:, 2:4, 0:384]
        a = act(ho(O2), op, ACT.Square, o["t_o"], o2_free)
        q = tt(G, Q2[:, :, :], U[r][:, 0:3, :], U[r][:, 0:3, :], ALU.mult, o["t_u"], q2_free)
        p, free = pairs.take()
        PE.wait(free, a, q)
        for par in range(2):
            mm(PSt[:, 4 + 2 * p + par, 0:384], C["ON"], O2[:, 3 * par:3 * par + 3, :], True, False)
        for par in range(2):
            w = slice(64 * par, 64 * par + 64)
            t = mm(PSt[:, 4 + 2 * p + par, 0:384], C["EP"][w, :], Q2[w, :, :], False, True, par == 1)
        o2_free, q2_free = [t], [t]
        a = act(ho(R), PSt[:, 4 + 2 * p:6 + 2 * p, 0:384], ACT.Ln, t, rr_free)
        pfree(p, a)
        a = act(R[:, :, :], R[:, :, :], ACT.Exp, a, scale=-0.5)
        a = tt(V, ho(OZ), op, ho(R), ALU.mult, a, oz_free)
        ofree = [a]
        rr_free = [a]
        a = tt(G, OZ[:, :, :], OZ[:, :, :], U[r][:, 9:15, :], ALU.mult, a)
        u_ring.free[r] = [a, o["t_o"], t]
        if u + 2 < 16:
            ul.append(load_u(u + 2))
        yield
        p, free = pairs.take()
        PE.wait(free, a, t_wo)
        for h_ in range(6):
            t = mm(bank(4 + 2 * p), OZ[:, h_, :], Wot[:, h_, :], h_ == 0, h_ == 5, h_ == 5)
        oz_free = [t]
        xr, t_x = xbl[u]
        k, free = x1_ring.take()
        a = tt(V, YB[k][:, :], bank(4 + 2 * p), gaB[:, b, :], ALU.mult, t, t_ga, free)
        pfree(p, a)
        a = tt(G, YB[k][:, :], YB[k][:, :], XB[xr][:, :], ALU.add, a, t_x)
        xb_ring.free[xr] = [a]
        t_r = rstd(u, YB[k][:, :], [a])
        t_x1[u] = x1_slots[k].start(SY, scrX[u], YB[k][:, :], a)
        x1_ring.free[k] = [t_x1[u], t_r]
        if u + 2 < 16:
            load_xb(u + 2)
        yield

    graw_slot = slots(1)[0]
    graw_free = []
    gw = Ring(4)

    def split_ff(r, t):
        nonlocal graw_free
        a = act(Ghi[r][:, :, :], Graw[:, :, :], ACT.Copy, t, gw.free[r])
        b_ = tt(V, Glo[r][:, :, :], Graw[:, :, :], Ghi[r][:, :, :].bitcast(f32), ALU.subtract, a, gw.free[r])
        graw_free = [b_]
        return b_

    def load_ff(j):
        t = graw_slot.start(SY, Graw[:, :, :], wg[j], graw_free)
        r, free = gw.take()
        return r, split_ff(r, t)

    fw = {}

    def weave(*gens):
        gens = [g_ for g_ in gens if g_ is not None]
        while gens:
            for g_ in list(gens):
                if next(g_, "end") == "end":
                    gens.remove(g_)

    weave(prep(0))
    for u in range(16):
        weave(rec(u), prep(u + 1) if u < 15 else None)
        weave(post(u))
        if u == 0:
            t_graw = graw_slot.start(SY, Graw[:, :, :], wg[0], allA, stores)
        if u == 1:
            fw[0] = (gw.take()[0], split_ff(0, t_graw))
            fw[1] = (gw.take()[0], graw_slot.start(SY, Graw[:, :, :], wg[1], graw_free))

    allB = [(E_.sem, E_.n) for E_ in (PE, V, SC, G)] + [x1_ring.free, xb_ring.free, u_ring.free]
    for E_ in (PE, V, SC, G, SY):
        E_.wait(allB)
    SC.q.append(lambda e: e.preload_act_table_set("silu_and_others"))
    hf_free[:] = [[], []]
    xn_free[:] = [[], []]
    pairs.free = [[], []]
    xf_slots, xc_slots, xc_ring = slots(4), slots(4), Ring(4)

    def load_xc(u, *w):
        r, free = xc_ring.take()
        return r, xc_slots[r].start(SY, XC[r][:, :], scrX[u], t_x1[u], free, *w)

    xf = [xf_slots[s].start(SY, XF[s][:, :], scrX[s * 4], t_x1[s * 4]) for s in range(4)]
    xl = {}
    t_hc = {}
    f_first = []

    def src_c(n):
        rd = []
        if n < 4:
            f_first.append(rd)
            return XF[n][:, :], xf[n], rd
        r, t = xl[n]
        xc_ring.free[r] = rd
        return XC[r][:, :], t, rd

    def norm_c():
        xc_ring.n = 2
        for n, _ in enumerate(norms(order, src_c, False, XNC, HFC, 2, 3, [t_sb, t_cb], Ring(1), 7, t_hc)):
            if 4 <= n + 1 < 16:
                xl[n + 1] = load_xc(order[n + 1])
            yield

    nrm = norm_c()
    for _ in range(8):
        next(nrm)
    t_gb = gate_rows(1, gbB)
    fw[1] = (1, split_ff(1, fw[1][1]))
    gub = Ring(4)
    yb = Ring(3)
    yb.free = [[pairs.free[0]], [], [pairs.free[1]]]
    si_ring, f_ring = Ring(2), Ring(4)
    f_ring.free = [list(r_) for r_ in f_first]
    gf_free = []
    t_y = {}
    outs = []
    xo = {}
    NG = 8

    def gate_up(q, b, step):
        nonlocal gf_free
        c = slice(b * SEQ, (b + 1) * SEQ)
        fs = []
        for jj in range(2):
            w, tw = fw[2 * q + jj]
            i1, free1 = gub.take()
            i2, free2 = gub.take()
            PE.wait(free1, free2, tw, t_hc[12 + b])
            for n, i in ((0, i1), (1, i2)):
                for k in range(4):
                    kk = slice(k * 128, (k + 1) * 128)
                    t = mm3(bank(i), Ghi[w][:, n, kk], Glo[w][:, n, kk], Hhi[:, k, c], Hlo[:, k, c], k == 0,
                            k == 3, k == 3)
                if n == 0:
                    z, free = si_ring.take()
                    t_si = act(SI[z][:, :], bank(i), ACT.Silu, t, free)
                    gub.free[i] = [t_si]
            a = tt(V, GF[:, :], bank(i2), SI[z][:, :], ALU.mult, t, t_si, gf_free)
            gub.free[i2] = [a]
            si_ring.free[z] = [a]
            k, free = f_ring.take()
            hi = act(FH[k][:, :], GF[:, :], ACT.Copy, a, free)
            lo = tt(V, FL[k][:, :], GF[:, :], FH[k][:, :].bitcast(f32), ALU.subtract, hi, free)
            gf_free = [lo]
            fs.append((k, w, lo))
            step()
        return fs

    def down(q, b, fs, step):
        for s in range(4):
            u = s * 4 + b
            i, free = yb.take()
            PE.wait(free, fs[0][2], fs[1][2])
            for n, (k, w, _) in enumerate(fs):
                tk = slice(s * 128, (s + 1) * 128)
                t = mm3(bank(4 + i), FH[k][:, tk], FL[k][:, tk], Ghi[w][:, 2, :], Glo[w][:, 2, :], n == 0, n == 1,
                        n == 1)
            if q == 0:
                t_y[u] = cp(V, yacc[:, u, :], bank(4 + i), t)
            else:
                t_y[u] = tt(V, yacc[:, u, :], bank(4 + i), yacc[:, u, :], ALU.add, t, t_y[u])
            yb.free[i] = [t_y[u]]
            if q == NG - 1:
                r, t_x = xo[u]
                a = tt(G, yacc[:, u, :], yacc[:, u, :], gbB[:, b, :], ALU.mult, t_y[u], t_gb)
                a = tt(G, yacc[:, u, :], yacc[:, u, :], XC[r][:, :], ALU.add, a, t_x)
                xc_ring.free[r] = [a]
                outs.append(Slot(sem()).start(SY, out[b, s * 128:(s + 1) * 128, :], yacc[:, u, :], a))
            step()
        for k, w, _ in fs:
            f_ring.free[k] = [t]
        if b == 3:
            for k, w, _ in fs:
                gw.free[w] = [t]

    pend = None
    for q in range(NG):
        for b in range(4):
            if q == 0 and b:
                while 12 + b not in t_hc:
                    next(nrm)
            fs = gate_up(q, b, (lambda: (next(nrm, None), next(nrm, None))) if (q, b) == (0, 0) else (lambda: None))
            if pend is not None:
                down(*pend, (lambda: next(nrm, None)) if q == 0 else (lambda: None))
            pend = (q, b, fs)
            if q == NG - 1:
                for s in range(4):
                    xo[s * 4 + b] = load_xc(s * 4 + b)
            if b == 1 and q + 1 < NG:
                for j in (2 * q + 2, 2 * q + 3):
                    fw[j] = load_ff(j)
            if q == 0 and b == 3:
                for _ in nrm:
                    pass
                yb.n, yb.i = 4, 2
                yb.free.append([t_hc[15]])
                xc_ring.n, xc_ring.free = 4, xc_ring.free[0:2] + [[t_hc[15]], [t_hc[15]]]
    down(*pend, lambda: None)
    SY.wait(outs)

    with nc.Block() as block:
        @block.sync
        def _(e):
            SY.run(e)

        @block.tensor
        def _(e):
            PE.run(e)

        @block.vector
        def _(e):
            V.run(e)

        @block.scalar
        def _(e):
            SC.run(e)

        @block.gpsimd
        def _(e):
            G.run(e)


def tiles(w, n):
    return np.ascontiguousarray(w.reshape(4, 128, n, 128).transpose(2, 1, 0, 3))


def kernel(**inputs):
    import concourse.bacc as bacc
    from concourse.bass_utils import run_bass_kernel_spmd

    v = {k: np.asarray(a) for k, a in inputs.items()}
    A = lambda n: v["L0_attn_" + n]
    wab = np.zeros((D, 128), np.float32)
    wab[:, 0:6] = A("Wa")[:, HEADS]
    wab[:, 6:12] = A("Wb")[:, HEADS]
    hv = lambda w: w.reshape(D, H, DV)[:, HEADS].reshape(D, H * DV)
    W1 = np.concatenate([tiles(wab, 1), tiles(A("Wk"), 3), tiles(A("Wq"), 3), tiles(hv(A("Wv")), 6),
                         tiles(hv(A("Wg")), 6)])
    cw = np.concatenate([A("conv_wk").reshape(3, 128, 4), A("conv_wq").reshape(3, 128, 4),
                         A("conv_wv").reshape(H, DV, 4)[HEADS]]).transpose(1, 0, 2)
    row = lambda a: np.broadcast_to(a[None, :], (128, H))
    gate, up = tiles(v["L0_ffn_w_gate"].T, 16), tiles(v["L0_ffn_w_up"].T, 16)
    down = v["L0_ffn_w_down"].T.reshape(16, 128, 1, D)
    arrays = {
        "x": v["L0_attn_hidden_states"],
        "W1": W1,
        "cw": cw,
        "dtb": row(A("dt_bias")[HEADS]),
        "alog": row(A("A_log")[HEADS]),
        "nw": A("norm_weight").reshape(128, 1),
        "Wo": A("Wo").reshape(H, DV, D)[HEADS].transpose(1, 0, 2),
        "cT": v["L0_c"].T.reshape(4, 128, 4).transpose(1, 0, 2),
        "wmod": v["L0_wmod"].reshape(4, 128, 6 * D).transpose(1, 0, 2),
        "wf": np.concatenate([gate.reshape(16, 128, 1, D), up.reshape(16, 128, 1, D), down], axis=2),
        "cst": constants(),
    }
    arrays = {k: np.ascontiguousarray(a) for k, a in arrays.items()}
    nc = bacc.Bacc("TRN2", target_bir_lowering=False, num_devices=1)
    h = {k: nc.dram_tensor("in_" + k, a.shape, mybir.dt.from_np(a.dtype), kind="ExternalInput").ap()
         for k, a in arrays.items()}
    out = nc.dram_tensor("out", (NB, SEQ, D), mybir.dt.float32, kind="ExternalOutput").ap()
    build(nc, h["x"], h["W1"], h["cw"], h["dtb"], h["alog"], h["nw"], h["Wo"], h["cT"], h["wmod"], h["wf"], h["cst"],
          out)
    r = run_bass_kernel_spmd(nc, [{"in_" + k: a for k, a in arrays.items()}], core_ids=[0])
    return r.results[0]["out"]
```

```python
import numpy as np
import concourse.bass as bass
from concourse import mybir

NB, SEQ, D, H, DK, DV, FF = 4, 512, 512, 6, 64, 128, 2048
NS = SEQ // 128
HEADS = [0, 2, 4, 1, 3, 5]
EPS = 1e-5
NT1 = 19
CONSTS = ["ident", "SG", "LE", "CH0", "CH1", "BO", "ON"]


def constants():
    i = np.arange(128)
    r, c = i[:, None], i[None, :]
    same = (r // 64) == (c // 64)
    m = {
        "ident": r == c,
        "SG": (r > c) & same,
        "LE": (r <= c) & same,
        "CH0": (r < 64) & (c >= 0),
        "CH1": (r >= 64) & (c >= 0),
        "BO": same,
        "ON": np.full((128, 128), 1.0 / 128),
    }
    cols = [m[n].astype(np.float32) for n in CONSTS]
    sel = np.zeros((128, NB * 128), np.float32)
    for b in range(NB):
        sel[b, b * 128:(b + 1) * 128] = 1.0
    extra = np.zeros((128, 8), np.float32)
    extra[:, 0] = EPS
    extra[:, 1] = 1.0
    return np.ascontiguousarray(np.concatenate(cols + [sel, extra], axis=1))


class Eng:

    def __init__(self, sem, serial=False):
        self.sem, self.n, self.q, self.seen, self.serial = sem, 0, [], {}, serial

    def wait(self, *toks):
        for t in toks:
            if t is None:
                continue
            if isinstance(t, (list, tuple)) and t and isinstance(t[0], (list, tuple)):
                self.wait(*t)
                continue
            if not t:
                continue
            sem, v = t
            if self.seen.get(id(sem), 0) < v:
                self.seen[id(sem)] = v
                self.q.append(lambda e, sem=sem, v=v: e.wait_ge(sem, v))

    def op(self, fn, *waits, inc=True):
        self.wait(*waits)
        if self.serial:
            self.wait((self.sem, self.n))
        if not inc:
            self.q.append(fn)
            return None
        self.n += 1
        self.q.append(lambda e: fn(e).then_inc(self.sem, 1))
        return (self.sem, self.n)

    def run(self, e):
        for f in self.q:
            f(e)


class Slot:

    def __init__(self, sem):
        self.sem, self.n = sem, 0

    def start(self, eng, out, in_, *waits):
        eng.wait(*waits)
        self.n += 16
        eng.q.append(lambda e: e.dma_start(out, in_).then_inc(self.sem, 16))
        return (self.sem, self.n)


class Ring:

    def __init__(self, n):
        self.n, self.i, self.free = n, -1, [[] for _ in range(n)]

    def take(self):
        self.i = (self.i + 1) % self.n
        return self.i, self.free[self.i]


def build(nc, x, W1, cw, dtb, alog, nw, Wo, cT, wmod, wg, cst, out):
    f32, f32r = mybir.dt.float32, mybir.dt.float32r
    ALU, ACT = mybir.AluOpType, mybir.ActivationFunctionType
    names = [0]

    def at(off, shape, dt=f32):
        names[0] += 1
        n = 4
        for s in shape[1:]:
            n *= s
        assert off % 32 == 0 and off + n <= 229216, (off, n)
        return nc.alloc_sbuf_tensor_at(f"t{names[0]}", shape, dt, offset=off)

    class Map:
        def __init__(self, base):
            self.p = base

        def new(self, shape, dt=f32):
            n = 4
            for s in shape[1:]:
                n *= s
            t = at(self.p, shape, dt)
            self.p += (n + 31) // 32 * 32
            return t

    scrU = nc.dram_tensor("scrU", (16, 128, 15, 128), f32).ap()
    scrA = nc.dram_tensor("scrA", (NS, 96, 32, 32), f32).ap()
    scrP = nc.dram_tensor("scrP", (NS, 96, 32, 32), f32).ap()
    scrX = nc.dram_tensor("scrX", (16, 128, D), f32).ap()

    M = Map(16384)
    NC_ = len(CONSTS) * 128
    cs = M.new([128, NC_ + 512 + 8])
    C = {n: cs[:, i * 128:(i + 1) * 128] for i, n in enumerate(CONSTS)}
    sel = cs[0:4, NC_:NC_ + 512]
    epsc, onec = cs[:, NC_ + 512:NC_ + 513], cs[:, NC_ + 513:NC_ + 514]
    ident = C["ident"]
    cwt = M.new([128, 12, 4])
    nwt = M.new([128, 1])
    dtbt, nexpA = M.new([128, H]), M.new([128, H])
    modT = M.new([128, 4, 4, NB])
    gnat = M.new([4, 2, D])
    g, nbeta, beta, nbg = (M.new([128, 16, H]) for _ in range(4))
    EX = M.new([128, NS, 4, 24])
    GC = M.new([128, NS, 2, NB, 3])
    mv, rs = M.new([128, 16, 2]), M.new([128, 16])
    st6 = M.new([128, 2, 6])
    kT = M.new([128, 3, NB * SEQ])
    P = M.new([128, NS, 24, 128])
    top = M.p
    A_ = Map(top)
    Hhi, Hlo = A_.new([128, NB, 4, SEQ], f32r), A_.new([128, NB, 4, SEQ], f32r)
    a_after_h = A_.p
    Wraw = [A_.new([128, 4, 128]) for _ in range(2)]
    Whi = [A_.new([128, 4, 128], f32r) for _ in range(2)]
    Wlo = [A_.new([128, 4, 128], f32r) for _ in range(2)]
    Y = [A_.new([128, SEQ]) for _ in range(2)]
    O = [A_.new([128, SEQ]) for _ in range(3)]
    Am = A_.new([128, NS, 24, 32])
    GMT = A_.new([128, H, 128])
    EV = A_.new([128, H, 128])
    Ab = [A_.new([128, H, 128]) for _ in range(2)]
    p3 = top - 24 * 128 * 4
    nAps, Pps = [A_.new([96, 32, 32]), at(p3, [96, 32, 32])], [A_.new([96, 32, 32]), at(p3 + 4096, [96, 32, 32])]
    tmps = [A_.new([96, 256]), at(p3 + 8192, [96, 256])]
    assert A_.p <= 229216, A_.p
    p_off = top - NS * 24 * 128 * 4
    S_ = Map(p_off)
    wm = [S_.new([128, 4, 512]) for _ in range(2)]
    modn = S_.new([4, 6, 512])
    X = [S_.new([128, D]) for _ in range(3)]
    XN = [S_.new([128, D]) for _ in range(2)]
    HF = [S_.new([128, 4, 128]) for _ in range(2)]
    cTt = S_.new([128, 4, 4])
    sgn = S_.new([4, 2, D])
    assert S_.p <= top
    w_off = a_after_h + 11 * 2048 + 24 * 512
    Wearly = [at(w_off + i * 2048, [128, 4, 128], f32r) for i in range(4)]
    WH, WL = Whi + Wearly[0:2], Wlo + Wearly[2:4]
    am_off = a_after_h + 11 * 2048
    ab = at(am_off, [12, NB * SEQ])
    zt = at(am_off + 8192, [128, 16, 12])
    z2 = at(am_off + 8192 + 768, [128, 16, H])
    z3 = at(am_off + 8192 + 768 + 384, [128, 16, H])
    B_ = Map(top)
    S = B_.new([128, NB * 3, 128])
    Sg = B_.new([128, 3, 128])
    U = [B_.new([128, 9, 128]) for _ in range(2)]
    UG = [B_.new([128, H, 128]) for _ in range(2)]
    UG_end = B_.p
    GMb, Eb = B_.new([128, H, 128]), B_.new([128, H, 128])
    Kbg, Kd, Qg = B_.new([128, 3, 2, 64]), [B_.new([128, 3, 2, 64]) for _ in range(2)], B_.new([128, 3, 2, 64])
    Vb = [B_.new([128, H, 128]) for _ in range(2)]
    QgT, WT = [B_.new([128, 3, 128]) for _ in range(2)], [B_.new([128, 3, 128]) for _ in range(2)]
    PAT = [B_.new([128, H, 128]) for _ in range(2)]
    dl = B_.new([128, H, 128])
    O2, R, OT, OZ = (B_.new([128, H, 128]) for _ in range(4))
    OZh, OZl = B_.new([128, H, 128], f32r), B_.new([128, H, 128], f32r)
    Q2 = [B_.new([128, 3, 128]) for _ in range(3)]
    XB = [B_.new([128, D]) for _ in range(2)]
    Woh = B_.new([128, H, D], f32r)
    wol_off = B_.p
    Wot = B_.new([128, H, D])
    Wol = at(wol_off, [128, H, D], f32r)
    gaB = B_.new([128, NB, D])
    YB = [B_.new([128, D]) for _ in range(2)]
    assert B_.p <= 229216, B_.p
    yb_off = B_.p - 4096
    c0 = Map(p_off - 3 * NB * SEQ * 4)
    SI = [c0.new([128, 512]) for _ in range(2)]
    gbB = c0.new([128, NB, D])
    XC = [c0.new([128, D]) for _ in range(2)]
    yacc2 = c0.new([128, 4, D])
    assert c0.p <= p_off
    c0 = Map(p_off)
    Graw = c0.new([128, 3, 512])
    Gb = [c0.new([128, 3, 512], f32r) for _ in range(3)]
    yacc = at(c0.p, [128, 12, D])
    assert c0.p + 12 * 2048 <= top
    c0 = Map(a_after_h)
    XNC = [c0.new([128, D]) for _ in range(2)]
    hfc_off = c0.p
    HFC = [c0.new([128, 4, 128]) for _ in range(2)]
    XC += [at(hfc_off + i * 2048, [128, D]) for i in range(2)]
    FH = [c0.new([128, 512], f32r) for _ in range(4)]
    FL = [c0.new([128, 512], f32r) for _ in range(4)]
    GF = c0.new([128, 512])
    Gb += [c0.new([128, 3, 512], f32r) for _ in range(5)]
    assert c0.p <= 229216, c0.p
    Ghi, Glo = [Gb[0], Gb[2], Gb[4], Gb[6]], [Gb[1], Gb[3], Gb[5], Gb[7]]

    XF = [yacc[:, i, :] for i in range(6)]

    assert yb_off >= c0.p - 6144, (yb_off, c0.p)

    def ya(u):
        return yacc[:, u, :] if u < 12 else yacc2[:, u - 12, :]

    PSt = nc.alloc_psum_tensor("ps", [128, 8, 512], f32)

    def bank(i):
        return PSt[:, i, :]

    def pair(i):
        return PSt[:, 2 * i:2 * i + 2, 0:384].rearrange("p a (m t) -> p a m t", m=3)

    def heads(t):
        return t.rearrange("p (a m) t -> p a m t", a=2)

    nsem = [0]

    def sem():
        nsem[0] += 1
        return nc.alloc_semaphore(f"s{nsem[0]}")

    PE, V, SC, SY = (Eng(sem()) for _ in range(4))
    G = Eng(sem(), serial=True)

    def slots(n):
        return [Slot(sem()) for _ in range(n)]

    def bc(ap, axis, shape):
        return ap.unsqueeze(axis).broadcast_to(shape)

    def mm(o, l, r, start, stop, last=False, *waits):
        return PE.op(lambda e: e.matmul(o, l, r, start=start, stop=stop, skip_group_check=True), *waits, inc=last)

    def mm3(o, lh, ll, rh, rl, first, stop, last=False):
        mm(o, lh, rh, first, False)
        mm(o, ll, rh, False, False)
        return mm(o, lh, rl, False, stop, last)

    def tr(o, i, idn, last=False, *waits):
        return PE.op(lambda e: e.transpose(o, i, idn), *waits, inc=last)

    def act(o, i, f, *waits, **k):
        return SC.op(lambda e: e.activation(o, i, f, **k), *waits)

    def tt(E, o, a, b, op, *waits):
        return E.op(lambda e: e.tensor_tensor(o, a, b, op), *waits)

    def ts(E, o, a, s1, s2, o1, o2, *waits):
        if s2 is None:
            return E.op(lambda e: e.tensor_scalar(o, a, s1, None, o1), *waits)
        return E.op(lambda e: e.tensor_scalar(o, a, s1, s2, o1, o2), *waits)

    def stt(o, a, s, b, o1, o2, *waits):
        return V.op(lambda e: e.scalar_tensor_tensor(o, a, s, b, o1, o2), *waits)

    def cp(E, o, i, *waits):
        return E.op(lambda e: e.tensor_copy(o, i), *waits)

    SC.q.append(lambda e: e.preload_act_table_set("silu_and_others"))
    k_c, k_cw, k_nw, k_dt, k_al, k_cT, k_id = slots(7)
    x_slots = slots(3)
    x_ring = Ring(3)

    def load_x(u):
        s, b = u // 4, u % 4
        r, free = x_ring.take()
        return r, x_slots[r].start(SY, X[r][:, :], x[b, s * 128:(s + 1) * 128, :], free)

    order = [s * 4 + b for b in range(4) for s in range(4)]
    xl = [load_x(order[0]), load_x(order[1])]
    t_id = k_id.start(SY, cs[:, 0:128], cst[:, 0:128])
    t_ep = k_c.start(SY, cs[:, NC_ + 512:NC_ + 520], cst[:, NC_ + 512:NC_ + 520])
    t_cT = k_cT.start(SY, cTt[:, :, :], cT)
    wm_slots = slots(2)
    wm_ring = Ring(2)
    t_wm = []

    def load_mod(i):
        r, free = wm_ring.take()
        t_wm.append((r, wm_slots[r].start(SY, wm[r][:, :, :], wmod[:, :, i * 512:(i + 1) * 512], free)))

    load_mod(0)
    load_mod(1)
    t_cst = Slot(sem()).start(SY, cs[:, 128:NC_ + 512], cst[:, 128:NC_ + 512])
    xl.append(load_x(order[2]))
    t_cw = k_cw.start(SY, cwt[:, :, :], cw)
    t_nw = k_nw.start(SY, nwt[:, :], nw)
    t_dt = k_dt.start(SY, dtbt[:, :], dtb)
    t_al = k_al.start(SY, nexpA[:, :], alog)

    tiles = [0, 9, 1, 10, 2, 11, 3, 12, 4, 13, 5, 14, 6, 7, 8]
    WSEQ = [0, 1, 2, 3] + [4 + n for n in tiles]
    w_slots = slots(2)
    w_ring = Ring(2)
    wh_ring = Ring(4)

    def load_w(j):
        r, free = w_ring.take()
        return r, w_slots[r].start(SY, Wraw[r][:, :, :], W1[WSEQ[j]], free)

    t_silu = act(cTt[:, :, :], cTt[:, :, :], ACT.Silu, t_cT)
    SC.q.append(lambda e: e.preload_act_table_set("natural_log_exp_and_others"))
    t_nexp0 = act(nexpA[:, :], nexpA[:, :], ACT.Exp, t_al)
    t_nexp = ts(V, nexpA[:, :], nexpA[:, :], -1.0, None, ALU.mult, None, t_nexp0)

    bfree = [[] for _ in range(8)]

    def split_w(j, ld):
        r, t = ld
        h, free = wh_ring.take()
        a = act(WH[h][:, :, :], Wraw[r][:, :, :], ACT.Copy, t, free)
        b = tt(V, WL[h][:, :, :], Wraw[r][:, :, :], WH[h][:, :, :].bitcast(f32), ALU.subtract, a, free)
        w_ring.free[r] = [b]
        return h, b

    def mod_rows(i):
        r, t = t_wm[i]
        bk = 7 - i % 2
        PE.wait(t, t_silu, bfree[bk])
        for k in range(4):
            tk = mm(bank(bk)[0:4, :], cTt[:, k, :], wm[r][:, k, :], k == 0, k == 3, k == 3)
        wm_ring.free[r] = [tk]
        if i in (1, 4):
            tm = ts(V, modn[:, i, :], bank(bk)[0:4, :], 1.0, None, ALU.add, None, tk)
        else:
            tm = cp(V, modn[:, i, :], bank(bk)[0:4, :], tk)
        bfree[bk] = [tm]
        return tm

    def mod_cols(i, dst, tm):
        PE.wait(tm, t_id, bfree[6])
        for k in range(4):
            tk = tr(bank(6)[:, k * 4:k * 4 + 4], modn[:, i, k * 128:(k + 1) * 128], ident[0:4, 0:4], k == 3)
        t = cp(V, modT[:, dst, :, :].rearrange("p k b -> p (k b)"), bank(6)[:, 0:16], tk)
        bfree[6] = [t]
        return t


    hf_free = [[], []]
    xn_free = [[], []]
    st_free = [[], []]

    def rstd(u, src, t_src):
        n = u % 2
        a = V.op(lambda e: e.bn_stats(st6[:, n, :], src), t_src, st_free[n])
        a = V.op(lambda e: e.bn_aggr(mv[:, u, :], st6[:, n, :]), a)
        st_free[n] = [a]
        l = act(rs[:, u:u + 1], mv[:, u, 1:2], ACT.Ln, a, bias=epsc)
        return act(rs[:, u:u + 1], rs[:, u:u + 1], ACT.Exp, l, scale=-0.5)

    def norms(us, src, stats, XNs, HFs, i_sh, i_sc, t_mod, ring, base, res, low=G):
        N, st = len(us), {}
        for n in range(N + 4):
            if n >= 4:
                u, o = us[n - 4], st[n - 4]
                b, c = u % 4, (u // 4) * 128
                lo = tt(low, Hlo[:, b, :, c:c + 128], HFs[o["m"]][:, :, :], Hhi[:, b, :, c:c + 128].bitcast(f32),
                        ALU.subtract, o["hi"])
                hf_free[o["m"]] = [lo]
                res[u] = lo
            if n >= 3 and n - 3 < N:
                u, o = us[n - 3], st[n - 3]
                b, m = u % 4, n % 2
                c = (u // 4) * 128
                hs = []
                for k in range(4):
                    i_, o_ = bank(o["bk"])[:, k * 128:(k + 1) * 128], HFs[m][:, k, :]
                    s1, s2 = modT[:, i_sc, k, b:b + 1], modT[:, i_sh, k, b:b + 1]
                    if n % 2 and not stats:
                        hs.append(ts(V, o_, i_, s1, s2, ALU.mult, ALU.add, o["tk"], t_mod, hf_free[m]))
                    else:
                        hs.append(act(o_, i_, ACT.Identity, o["tk"], t_mod, hf_free[m], scale=s1, bias=s2))
                ring.free[o["r"]] = [hs[3]]
                o["hi"] = act(Hhi[:, b, :, c:c + 128], HFs[m][:, :, :], ACT.Copy, hs[3])
                o["m"] = m
            if n >= 2 and n - 2 < N:
                o = st[n - 2]
                m = n % 2
                o["r"], free = ring.take()
                o["bk"] = base + o["r"]
                PE.wait(o["xn"], free, t_id)
                src_n = XNs[m][:, :] if o["rd"] is not None else o["x"]
                for k in range(4):
                    tk = tr(bank(o["bk"])[:, k * 128:(k + 1) * 128], src_n[:, k * 128:(k + 1) * 128], ident, k == 3)
                if o["rd"] is not None:
                    xn_free[m] = [tk]
                o["tk"] = tk
            if n >= 1 and n - 1 < N:
                u, o = us[n - 1], st[n - 1]
                m = (n + 1) % 2
                o["xn"] = o["l"] if o["rd"] is None else ts(V, XNs[m][:, :], o["x"], mv[:, u, 0:1], rs[:, u:u + 1], ALU.subtract, ALU.mult, o["l"],
                             xn_free[m])
                if o["rd"] is not None:
                    o["rd"].append(o["xn"])
            if n < N:
                xt, t, rd = src(n)
                st[n] = {"x": xt, "l": rstd(us[n], xt, [t, t_ep]) if stats else t, "rd": rd}
            yield

    wl = [load_w(0), load_w(1)]

    def src_x(n):
        r, t = xl[n]
        rd = []
        x_ring.free[r] = rd
        return X[r][:, :], t, rd

    t_hn = {}
    n_ring = Ring(2)
    t_m = []

    def norm_x():
        for n, _ in enumerate(norms(order, src_x, True, XN, HF, 0, 1, t_m, n_ring, 4, t_hn)):
            if 3 <= n + 2 < 16:
                xl.append(load_x(order[n + 2]))
            yield

    nrm = norm_x()
    next(nrm)
    next(nrm)
    m0, m1 = mod_rows(0), mod_rows(1)
    t_m += [mod_cols(0, 0, m0), mod_cols(1, 1, m1)]
    for _ in range(6):
        next(nrm)
    load_mod(2)
    load_mod(3)

    def late_mods(early):
        tms = early + [mod_rows(4), mod_rows(5)]
        t_sb, t_cb = mod_cols(3, 2, tms[1]), mod_cols(4, 3, tms[2])
        for n, i in ((0, 2), (1, 5)):
            src = modn[:, i, :]
            a = stt(gnat[:, n, :], src, -1.0, src, ALU.mult, ALU.max, tms[i - 2])
            a = ts(V, gnat[:, n, :], gnat[:, n, :], 0.25, None, ALU.max, None, a)
            c_ = ts(V, sgn[:, n, :], src, 0.0, 2.0, ALU.is_ge, ALU.mult, a)
            c_ = ts(V, sgn[:, n, :], sgn[:, n, :], -1.0, None, ALU.add, None, c_)
            t = tt(V, gnat[:, n, :], gnat[:, n, :], sgn[:, n, :], ALU.mult, c_)
        return t_sb, t_cb, t

    pr = Ring(4)

    def project(h, tw, b):
        i, free = pr.take()
        PE.wait(free, tw, t_hn[12 + b])
        for k in range(4):
            t = mm3(bank(i), WH[h][:, k, :], WL[h][:, k, :], Hhi[:, b, k, :], Hlo[:, b, k, :], k == 0, k == 3, k == 3)
        return i, t

    y_ring, o_ring = Ring(2), Ring(3)
    o_slots = slots(3)

    def conv(i, t, j, dst=None, between=lambda: None):
        y, free = y_ring.take() if dst is None else (None, [])
        p, yy = bank(i), Y[y] if dst is None else dst
        w = lambda n: cwt[:, j, n:n + 1]
        a = act(yy[:, :], p, ACT.Copy, t, free, t_cw, scale=w(3))
        for n in (2, 1, 0):
            d = 3 - n
            a = stt(yy[:, d:SEQ], p[:, 0:SEQ - d], w(n), yy[:, d:SEQ], ALU.mult, ALU.add, a)
            between()
        pr.free[i] = [a]
        return y, a

    t_scrU = {}

    def store_unit(o, t, tile, b):
        dst = scrU.rearrange("(s b) p j t -> b j p s t", b=4)[b, tile]
        src = O[o][:, :].rearrange("p (s t) -> p s t", s=4)
        tk = o_slots[o].start(SY, dst, src, t)
        o_ring.free[o] = [tk]
        t_scrU[(tile, b)] = tk

    def next_w(j):
        got_w = split_w(j, wl[j])
        if j + 2 < NT1:
            wl.append(load_w(j + 2))
        return got_w

    hw = [next_w(j) for j in range(4)]
    t_k = {}
    ahead = [project(*hw[0], 0)]
    for b in range(4):
        for m in range(4):
            if (b, m) == (3, 0):
                wh_ring.free[0] = [ahead[-1][1]]
                nxt = next_w(4)
            if (b, m) != (3, 3):
                while 12 + b + (m == 3) not in t_hn:
                    next(nrm)
                ahead.append(project(*hw[(m + 1) % 4], b + (m == 3)))
            i, t = ahead.pop(0)
            if m == 0:
                t_ab = cp(V, ab[:, b * SEQ:(b + 1) * SEQ], bank(i)[0:12, :], t)
                pr.free[i] = [t_ab]
            else:
                _, t_k[(m - 1, b)] = conv(i, t, m - 1, kT[:, m - 1, b * SEQ:(b + 1) * SEQ])
            next(nrm, None)
        if b == 1:
            early = [mod_rows(2), mod_rows(3)]
            load_mod(4)
            load_mod(5)
    wh_ring = Ring(2)
    wh_ring.i, wh_ring.free = 0, [[t], [t]]
    SQ = [at(w_off, [128, 3, SEQ]), at(w_off + 6144, [128, 3, SEQ])]
    sq_free = [[t], [t]]
    SC.q.append(lambda e: e.preload_act_table_set("silu_and_others"))
    PE.wait(t_ab, t_id, t_cst, bfree[7])
    for u in range(16):
        s, b = u // 4, u % 4
        tk = tr(bank(7)[:, u * 12:u * 12 + 12], ab[:, b * SEQ + s * 128:b * SEQ + s * 128 + 128],
                ident[0:12, 0:12], u == 15)
    t_z = cp(V, zt[:, :, :].rearrange("p u c -> p (u c)"), bank(7)[:, 0:192], tk)
    bfree[7] = [t_z]
    SC.q.append(lambda e: e.preload_act_table_set("natural_log_exp_and_others"))
    sh = [128, 16, H]
    t_a = tt(V, zt[:, :, 0:6], zt[:, :, 0:6], bc(dtbt[:, :], 1, sh), ALU.add, t_z, t_dt)
    a = act(z2[:, :, :], zt[:, :, 0:6], ACT.Abs, t_a)
    a = act(z2[:, :, :], z2[:, :, :], ACT.Exp, a, scale=-1.0)
    a = act(z2[:, :, :], z2[:, :, :], ACT.Ln, a, bias=onec)
    a = stt(z3[:, :, :], zt[:, :, 0:6], 0.0, z2[:, :, :], ALU.max, ALU.add, a)
    t_g = tt(V, g[:, :, :], z3[:, :, :], bc(nexpA[:, :], 1, sh), ALU.mult, a, t_nexp)
    a = act(z2[:, :, :], zt[:, :, 6:12], ACT.Exp, a, scale=-1.0)
    a = ts(V, z2[:, :, :], z2[:, :, :], 1.0, None, ALU.add, None, a)
    t_be = V.op(lambda e: e.reciprocal(beta[:, :, :], z2[:, :, :]), a)
    t_nb = ts(V, nbeta[:, :, :], beta[:, :, :], -1.0, None, ALU.mult, None, t_be)
    t_kb, t_sq = {}, {}
    mods = {}
    setup_done = [list(t_hn.values()), xn_free, hf_free]

    def k_square(b):
        kk = kT[:, :, b * SEQ:(b + 1) * SEQ]
        a = act(kk, kk, ACT.Silu, [t_k[(m, b)] for m in range(3)])
        t_sq[b] = tt(V, SQ[b % 2][:, :, :], kk, kk, ALU.mult, a, sq_free[b % 2])

    def k_norm():
        k_square(0)
        yield
        for b in range(4):
            y = SQ[b % 2]
            kk = kT[:, :, b * SEQ:(b + 1) * SEQ]
            if b < 3:
                k_square(b + 1)
            PE.wait(t_sq[b], t_cst, pairs.free)
            for m in range(3):
                t = mm(bank(4 + m), C["BO"], y[:, m, :], True, True, m == 2)
            SC.q.append(lambda e: e.preload_act_table_set("natural_log_exp_and_others"))
            a = act(y[:, :, :], PSt[:, 4:7, :], ACT.Ln, t)
            t_ln = a
            pairs.free = [[a], [a]]
            a = act(y[:, :, :], y[:, :, :], ACT.Exp, a, scale=-0.5)
            SC.q.append(lambda e: e.preload_act_table_set("silu_and_others"))
            t_kb[b] = tt(V, kk, kk, y[:, :, :], ALU.mult, a)
            sq_free[b % 2] = [t_kb[b]]
            if b == 2:
                bfree[:] = [[t_ln]] * 8
                mods["sb"], mods["cb"], mods["gn"] = late_mods(early)
                setup_done.append(list(mods.values()))
                pairs.free = [[t_ln], bfree[6] + bfree[7]]
            yield


    pairs = Ring(2)
    pairs.free = [[bfree[4], bfree[5], n_ring.free], [bfree[6], bfree[7]]]

    def pfree(i, t):
        pairs.free[i] = [t]

    ab_ring = Ring(2)
    a_slots = [slots(4), slots(4)]
    for q in (0, 64):
        t_am0 = G.op(lambda e, q=q: e.memset(Am[q:q + 32, :, :, :], 0.0), t_g, t_nb, t_z)
    t_am = {}
    t_ex, a_out, t_pz, din, t_P = {}, {}, {}, {}, {}
    gms = [GMT, EV, Ab[0], Ab[1]]
    gm_free, ev_free = [], []

    def decay_mult(E, u, GMx, free_gm, w="SG"):
        return tt(E, GMx[:, :, :], bc(C[w], 1, [128, H, 128]), bc(g[:, u, :], 2, [128, H, 128]), ALU.mult,
                  t_g, t_cst, free_gm)

    def decay_exp(a, GMx, Ex, free_e, w="LE"):
        p, free = pairs.take()
        PE.wait(a, free)
        for par in range(2):
            t = mm(PSt[:, 4 + 2 * p + par, 0:384], C[w], GMx[:, 3 * par:3 * par + 3, :], True, True, par == 1)
        e = act(heads(Ex), pair(2 + p), ACT.Exp, t, free_e)
        pfree(p, e)
        return t, e

    t_e2 = []

    def sums(s):
        p, free = pairs.take()
        bk = bank(4 + 2 * p)
        rhs = g[:, 4 * s:4 * s + 4, :].rearrange("p u h -> p (u h)")
        PE.wait(free, t_g, t_cst)
        for n, w in enumerate(("LE", "SG", "CH0", "CH1")):
            t = mm(bk[:, n * 24:n * 24 + 24], C[w], rhs, n == 0, True, n == 3)
        e = act(EX[:, s, :, :].rearrange("p n h -> p (n h)"), bk[:, 0:96], ACT.Exp, t)
        pfree(p, e)
        v = EX[:, s, :, :].rearrange("p n (b a m) -> p n b a m", b=4, a=2)
        for par in range(2):
            q = slice(64 * par, 64 * par + 64)
            for c in range(2):
                a = cp(V, GC[q, s, c, :, :], v[q, 2 + c, :, par, :], e)
        w = tt(V, nbg[:, 4 * s:4 * s + 4, :].rearrange("p u h -> p (u h)"),
               nbeta[:, 4 * s:4 * s + 4, :].rearrange("p u h -> p (u h)"), EX[:, s, 0, :], ALU.mult, e, t_nb)
        t_ex[s] = w

    def inverse_1(s):
        nonlocal gm_free, ev_free, t_e2
        e_free = setup_done if s < 3 else t_e2
        if s == 0:
            gm_free, ev_free = [t_kb[3], t_kb[2]], [t_kb[3], t_kb[2]]
            ab_ring.free = [gm_free, gm_free]
        se = min(s, 2)
        gf = [gm_free, ev_free, ab_ring.free[0], ab_ring.free[1]]
        gm = [decay_mult(G if b % 2 else V, s * 4 + b, gms[b], gf[b]) for b in range(4)]
        yield
        yield
        SC.q.append(lambda e: e.preload_act_table_set("natural_log_exp_and_others"))
        E = []
        for b in range(4):
            t, e = decay_exp(gm[b], gms[b], P[:, se, b * 6:b * 6 + 6, :], e_free)
            E.append(e)
        gm_free, ev_free = [t], [t]
        ab_ring.free = [[t], [t]]
        sums(s)
        SC.q.append(lambda e: e.preload_act_table_set("silu_and_others"))
        yield
        toks, am = [], []
        for b in range(4):
            u = s * 4 + b
            p, free = pairs.take()
            PE.wait(free, t_kb[b])
            for m in range(3):
                for par in range(2):
                    r = slice(64 * par, 64 * par + 64)
                    kk = kT[r, m, b * SEQ + s * 128:b * SEQ + s * 128 + 128]
                    t = mm(PSt[:, 4 + 2 * p + par, m * 128:m * 128 + 128], kk, kk, True, True, m == 2 and par == 1)
            i, free = ab_ring.take()
            PSp = pair(2 + p)
            V.wait(t, E[b], free, t_nb)
            for h_ in range(6):
                ev = a = stt(Ab[i][:, h_, :], PSp[:, h_ // 3, h_ % 3, :], nbeta[:, u, h_:h_ + 1],
                             P[:, se, b * 6 + h_, :], ALU.mult, ALU.mult)
            pfree(p, a)
            for c in range(2):
                q = slice(64 * c + 32, 64 * c + 64)
                t = act(Am[q, s, b * 6:b * 6 + 6, :], Ab[i][q, :, 64 * c:64 * c + 32], ACT.Copy, a, t_am0)
            am.append(t)
            d = []
            for k in range(4):
                q = slice(32 * k, 32 * k + 32)
                d.append(a_slots[i][k].start(SY, scrA[s, k * 24 + b * 6:k * 24 + b * 6 + 6].rearrange("h t i -> t h i"),
                                             Ab[i][q, :, q], a))
            ab_ring.free[i] = [am[-1]] + d
            toks += d
            if b == 3:
                a_out[s], t_am[s] = toks, am
                t_e2 = [ev]
                if s != 2:
                    t_pz[se] = G.op(lambda e: e.memset(P[:, se, :, :], 0.0), ev)
            yield

    nap_slots, pp_slots = slots(2), slots(2)
    pin_slots = slots(4)
    pp_free = [[], setup_done]

    def inverse_2(s, E, x):
        nAp, Pp, tmp = nAps[x], Pps[x], tmps[x]
        t = nap_slots[x].start(SY, nAp[:, :, :], scrA[s], a_out[s], pp_free[x])
        a = G.op(lambda e: e.memset(Pp[:, :, :], 0.0), pp_free[x])
        dg = Pp[:, :, :].rearrange("p a b -> p (a b)")[:, 0:1024:33]
        a = G.op(lambda e: e.memset(dg, 1.0), a)
        for _ in range(10):
            yield
        E.wait(t)
        for j in range(31):
            n, w = j + 1, 31 - j
            tm = tmp[:, 0:n * w].rearrange("p (c t) -> p c t", c=n)
            a = tt(E, tm, Pp[:, 0:n, j:j + 1].broadcast_to([96, n, w]),
                   bc(nAp[:, j + 1:32, j], 1, [96, n, w]), ALU.mult, a)
            yield
            a = tt(E, Pp[:, 0:n, j + 1:32], Pp[:, 0:n, j + 1:32], tm, ALU.add, a)
            yield
        o = pp_slots[x].start(SY, scrP[s], Pp[:, :, :], a)
        if s == 2:
            t_pz[3] = G.op(lambda e: e.memset(P[:, 3, :, :], 0.0), o)
        pp_free[x] = [a, o]
        din[s] = []
        for k in range(4):
            q = slice(32 * k, 32 * k + 32)
            din[s].append(pin_slots[k].start(SY, P[q, s, :, q],
                                             scrP[s, k * 24:k * 24 + 24].rearrange("h c t -> c h t"), o, t_pz[s]))

    def merge(s):
        nonlocal gm_free, ev_free
        t_e0 = V.op(lambda e: e.memset(EV[:, :, :], 0.0), ev_free)
        ev_free = [t_e0]
        for b in range(5):
            if b:
                hb = slice(b * 6 - 6, b * 6)
                p, free = pairs.take()
                PE.wait(free, v, tT)
                for h_ in range(6):
                    t2 = mm(PSt[:, 4 + 2 * p + h_ // 3, (h_ % 3) * 64:(h_ % 3) * 64 + 64], GMT[:, h_, :],
                            EV[:, h_, :].rearrange("p (c t) -> p c t", c=2)[:, :, 32:64], True, True, h_ == 5)
                gm_free, ev_free = [t2], [t2]
                for c in range(2):
                    q, w = slice(64 * c, 64 * c + 32), slice(64 * c + 32, 64 * c + 64)
                    src = PSt[q, 4 + 2 * p:6 + 2 * p, 0:192].rearrange("p a (m c t) -> p a m c t", m=3, c=2)[:, :, :, c, :]
                    a = cp(V, heads(P[:, s, hb, :])[q, :, :, w], src, t2, tT)
                pfree(p, a)
                t_P[(s, b - 1)] = a
            if b < 4:
                hb = slice(b * 6, b * 6 + 6)
                tT = V.op(lambda e, hb=hb: e.transpose(GMT[:, :, :], P[:, s, hb, :]), din[s], t_pz[s], gm_free)
                p, free = pairs.take()
                PE.wait(free, din[s], t_pz[s], t_am[s][b])
                for c in range(2):
                    for h_ in range(6):
                        t = mm(PSt[64 * c:64 * c + 32, 4 + 2 * p + c, h_ * 32:h_ * 32 + 32],
                               Am[:, s, b * 6 + h_, :], P[:, s, b * 6 + h_, 64 * c + 32:64 * c + 64], True, True,
                               h_ == 5)
                for c in range(2):
                    q, w = slice(64 * c, 64 * c + 32), slice(64 * c + 32, 64 * c + 64)
                    v = act(EV[q, :, w], PSt[q, 4 + 2 * p + c, 0:192].rearrange("p (h t) -> p h t", h=6), ACT.Copy, t,
                            ev_free)
                pfree(p, v)
            yield

    lanes = [[(0, 1, k_norm()), (5, 1, inverse_1(0)), (12, 1, inverse_1(1)), (19, 1, inverse_1(2)),
              (26, 1, inverse_1(3)), (33, 1, merge(0)), (39, 1, merge(1)), (49, 1, merge(2)), (54, 1, merge(3))],
             [(12, 5, inverse_2(0, V, 0)), (34, 5, inverse_2(3, V, 0))],
             [(19, 5, inverse_2(1, G, 1)), (34, 6, inverse_2(2, G, 1))]]
    running = [None] * 3
    left = [0] * 3

    def begin(slot):
        for l, lane in enumerate(lanes):
            if running[l] is None and lane and lane[0][0] <= slot:
                running[l] = lane.pop(0)
            left[l] = running[l][1] if running[l] else 0

    def side(l, n=99):
        while running[l] and left[l] and n:
            left[l] -= 1
            n -= 1
            if next(running[l][2], "end") == "end":
                running[l] = None
                if lanes[l] and lanes[l][0][0] <= slot:
                    running[l] = lanes[l].pop(0)
                    left[l] += 1

    u_slots, u_ring, g_slots, g_ring = slots(2), Ring(2), slots(2), Ring(2)
    xb_slots, xb_ring = slots(2), Ring(2)
    ul, gl, xbl, got = {}, {}, {}, {}

    def load_u(u):
        r, free = u_ring.take()
        ul[u] = (r, u_slots[r].start(SY, U[r][:, :, :], scrU[u, :, 0:9], p_end, stores(u, 0, 9), free))

    def load_g(u):
        r, free = g_ring.take()
        gl[u] = (r, g_slots[r].start(SY, UG[r][:, :, :], scrU[u, :, 9:15], p_end, stores(u, 9, 15), free))

    def stores(u, lo, hi):
        return [t_scrU[(k, u % 4)] for k in range(lo, hi)]

    slot = 0
    SC.q.append(lambda e: e.preload_act_table_set("silu_and_others"))
    ahead = [project(*nxt, 0)]
    for n, tile in enumerate(tiles):
        for b in range(4):
            begin(slot)
            h = nxt[0]
            if b == 0 and n < 14:
                nxt_ = next_w(5 + n)
            if b < 3:
                ahead.append(project(*nxt, b + 1))
                if (n, b) == (14, 1):
                    p_end = ahead[-1][1]
                if b == 2:
                    wh_ring.free[h] = [ahead[-1][1]]
                    if n < 14:
                        nxt = nxt_
            elif n < 14:
                ahead.append(project(*nxt, 0))
            i, t = ahead.pop(0)
            o, free = o_ring.take()
            if tile >= 9:
                a = act(O[o][:, :], bank(i), ACT.Silu, t, free)
                pr.free[i] = [a]
            else:
                y, a = conv(i, t, 3 + tile, between=lambda: side(1, 1))
                a = act(O[o][:, :], Y[y][:, :], ACT.Silu, a, free)
                y_ring.free[y] = [a]
            store_unit(o, a, tile, b)
            if (n, b) == (14, 2):
                load_u(0)
                load_g(0)
                load_u(1)
            side(0)
            side(1)
            side(2)
            slot += 1
    while any(running) or any(lanes):
        begin(99)
        for l in range(3):
            side(l)
    t_sb, t_cb, t_gn = mods["sb"], mods["cb"], mods["gn"]
    SC.q.append(lambda e: e.preload_act_table_set("natural_log_exp_and_others"))

    o_done = list(o_ring.free)
    allA = [(E_.sem, E_.n) for E_ in (PE, V, SC, G)]
    def load_xb(u):
        s, b = u // 4, u % 4
        r, free = xb_ring.take()
        xbl[u] = (r, xb_slots[r].start(SY, XB[r][:, :], x[b, s * 128:(s + 1) * 128, :], allA, o_done, free))

    t_wo = slots(1)[0].start(SY, Wot[:, :, :], Wo, allA, o_done)
    load_g(1)
    load_xb(0)
    load_xb(1)
    for E_ in (V, SC, G):
        E_.wait(allA)
    t_s0 = G.op(lambda e: e.memset(S[:, :, :], 0.0))
    t_d0 = G.op(lambda e: e.memset(dl[:, :, :], 0.0))

    def gate_rows(n, dst, step=2):
        for b in range(NB):
            p, free = pairs.take()
            bk = bank(4 + step * p)
            t = mm(bk, sel[:, b * 128:(b + 1) * 128], gnat[:, n, :], True, True, True, free, t_gn)
            a = act(dst[:, b, :], bk, ACT.Copy, t)
            pfree(p, a)
        return a

    def setup_b():
        o["t_ga"] = gate_rows(0, gaB)
        yield
        for h_ in (0, 2, 4):
            w, wh, wl_ = Wot[:, h_:h_ + 2, :], Woh[:, h_:h_ + 2, :], Wol[:, h_:h_ + 2, :]
            a = act(w, w, ACT.Copy, t_wo, t_nw, scale=nwt[:, 0:1])
            a = act(wh, w, ACT.Copy, a, o_done)
            o["t_wo"] = tt(G, wl_, w, wh.bitcast(f32), ALU.subtract, a)
            yield

    o = {}
    assert UG_end <= top + 3 * 8192
    st = {k: [] for k in ("gmb", "eb", "kbg", "qg", "pan", "sg", "d", "o", "o2", "r", "ot", "oz", "ozs")}
    r2 = {n: Ring(2) for n in ("Kd", "Vb", "QgT", "WT", "PAT")}
    r2["Q2"] = Ring(3)
    r2["Q2"].free = [[o_done] for _ in range(3)]
    st["d"], st["o"] = [pr.free[0], pr.free[1]], [pr.free[2], pr.free[3]]
    t_S = {b: t_s0 for b in range(NB)}

    def prep(u):
        s, b = u // 4, u % 4
        r, t_u = ul[u]
        col = slice(b * SEQ + s * 128, b * SEQ + s * 128 + 128)
        sc_ = lambda ap: bc(ap.rearrange("p (a m) -> p m a", a=2), 3, [128, 3, 2, 64])
        ex = lambda n: EX[:, s, n, b * 6:b * 6 + 6]
        q3 = lambda bk: bk[:, 0:384].rearrange("p (m a t) -> p m a t", m=3, a=2)
        o = {}
        gm = decay_mult(V, u, GMb, st["gmb"], "LE")
        p, free = pairs.take()
        PE.wait(free)
        for m in range(3):
            t0 = tr(bank(4 + 2 * p)[:, m * 128:m * 128 + 128], kT[:, m, col], ident, m == 2)
        PE.wait(t_u)
        for m in range(3):
            t = tr(bank(5 + 2 * p)[:, m * 128:m * 128 + 128], U[r][:, m, :], ident, m == 2)
        n_, free = r2["Kd"].take()
        o["Kd"] = n_
        t_kbg = tt(V, Kbg[:, :, :, :], q3(bank(4 + 2 * p)), sc_(nbg[:, u, :]), ALU.mult, t0, t_ex[s], st["kbg"])
        o["t_kd"] = tt(V, Kd[n_][:, :, :, :], q3(bank(4 + 2 * p)), sc_(ex(1)), ALU.mult, free)
        t_qg = tt(V, Qg[:, :, :, :], q3(bank(5 + 2 * p)), sc_(ex(0)), ALU.mult, t, st["qg"])
        pfree(p, t_qg)
        n_, free = r2["Q2"].take()
        o["Q2"] = n_
        o["t_q2"] = stt(Q2[n_][:, :, :], U[r][:, 0:3, :], 128.0 * EPS * DK, U[r][:, 0:3, :], ALU.mult, ALU.mult, t_u,
                        free)
        yield
        gm, e = decay_exp(gm, GMb, Eb[:, :, :], st["eb"], "SG")
        st["gmb"] = [gm]
        le = bc(C["LE"], 1, [128, H, 128])
        e = tt(G, Eb[:, :, :], Eb[:, :, :], le, ALU.mult, e)
        yield
        p, free = pairs.take()
        PE.wait(free)
        for h_ in range(6):
            t = tr(PSt[:, 4 + 2 * p + h_ // 3, (h_ % 3) * 128:(h_ % 3) * 128 + 128], U[r][:, 3 + h_, :], ident, h_ == 5)
        n_, free = r2["Vb"].take()
        o["Vb"] = n_
        o["t_vb"] = tt(V, heads(Vb[n_][:, :, :]), pair(2 + p),
                       bc(beta[:, u, :].rearrange("p (a m) -> p a m", a=2), 3, [128, 2, 3, 128]), ALU.mult, t, free)
        pfree(p, o["t_vb"])
        yield
        p, free = pairs.take()
        PE.wait(free)
        for m in range(3):
            for par in range(2):
                q = slice(64 * par, 64 * par + 64)
                t = mm(PSt[:, 4 + 2 * p + par, m * 128:m * 128 + 128], kT[q, m, col], U[r][q, m, :], True, True,
                       m == 2 and par == 1)
        u_ring.free[r] = [t, o["t_q2"]]
        if u + 2 < 16:
            load_u(u + 2)
        n_, free = r2["PAT"].take()
        o["PAT"] = n_
        o["t_pat"] = tt(V, heads(PAT[n_][:, :, :]), pair(2 + p), heads(Eb[:, :, :]), ALU.mult, t, e, free)
        pfree(p, o["t_pat"])
        st["eb"] = [o["t_pat"]]
        yield
        p, free = pairs.take()
        PE.wait(free, t_qg, t_kbg, t_P[(s, b)])
        for m in range(3):
            tr(bank(4 + 2 * p)[:, m * 128:m * 128 + 128], Qg[:, m, :, :].rearrange("p a t -> p (a t)"), ident)
        for m in range(3):
            for par in range(2):
                t = mm(PSt[64 * par:64 * par + 64, 5 + 2 * p, m * 128:m * 128 + 128], Kbg[:, m, par, :],
                       P[:, s, b * 6 + par * 3 + m, :], True, True, m == 2 and par == 1)
        st["kbg"], st["qg"] = [t], [t]
        n_, free = r2["QgT"].take()
        o["QgT"] = n_
        act(QgT[n_][:, :, :].rearrange("p m t -> p (m t)"), bank(4 + 2 * p)[:, 0:384], ACT.Copy, t, free)
        n_, free = r2["WT"].take()
        o["WT"] = n_
        o["t_wt"] = act(WT[n_][:, :, :].rearrange("p m t -> p (m t)"), bank(5 + 2 * p)[:, 0:384], ACT.Copy, free)
        pfree(p, o["t_wt"])
        got[u] = o
        yield

    dl_w = [[t_d0], [t_d0]]
    dl_r = [[], []]
    ho = lambda t: t[:, :, :].rearrange("p (a m) t -> p a (m t)", a=2)

    def rec(u):
        s, b = u // 4, u % 4
        o = got[u]
        kd, vb, qg, wt, pa = Kd[o["Kd"]], Vb[o["Vb"]], QgT[o["QgT"]], WT[o["WT"]], PAT[o["PAT"]]
        PE.wait(st["d"], o["t_vb"], t_P[(s, b)])
        for m in range(3):
            for par in range(2):
                h_ = par * 3 + m
                mm(PSt[:, par, m * 128:m * 128 + 128], P[:, s, b * 6 + h_, :], vb[:, h_, :], m == 0, True)
        PE.wait(o["t_wt"])
        for c in range(2):
            q = slice(64 * c, 64 * c + 64)
            PE.wait(t_S[b])
            for m in range(3):
                for par in range(2):
                    w = slice(64 * par, 64 * par + 64)
                    t = mm(PSt[q, par, m * 128:m * 128 + 128], wt[w, m, q], S[w, b * 3 + m, :], False, True,
                           m == 2 and par == 1)
            t_dl = act(heads(dl[:, :, :])[q], pair(0)[q], ACT.Copy, t, dl_w[c], dl_r[0], dl_r[1])
            gcv = GC[:, s, c, b, :]
            t_sg = tt(G, Sg[:, :, :], S[:, b * 3:b * 3 + 3, :], bc(gcv, 2, [128, 3, 128]), ALU.mult, t_S[b], st["sg"],
                      t_ex[s])
            if c == 0:
                PE.wait(st["o"])
            for m in range(3):
                for par in range(2):
                    w = slice(64 * par, 64 * par + 64)
                    t_o1 = mm(PSt[:, 2 + par, m * 128 + 64 * c:m * 128 + 64 * c + 64], S[w, b * 3 + m, :],
                              qg[w, m, q], c == 0 and m == 0, True, m == 2 and par == 1)
            yield
            p, free = pairs.take()
            PE.wait(free, t_dl, o["t_kd"], o["t_pat"])
            for m in range(3):
                for par in range(2):
                    w = slice(64 * par, 64 * par + 64)
                    t_s = mm(PSt[w, 4 + 2 * p, m * 128:m * 128 + 128], kd[q, m, par, :], dl[q, par * 3 + m, :],
                             True, True, m == 2 and par == 1)
            a = tt(V, S[:, b * 3:b * 3 + 3, :], Sg[:, :, :],
                   bank(4 + 2 * p)[:, 0:384].rearrange("p (m t) -> p m t", m=3), ALU.add, t_s, t_sg, t_o1)
            t_S[b] = a
            st["sg"] = [a]
            pfree(p, a)
            if c == 0:
                yield
        for m in range(3):
            for par in range(2):
                h_ = par * 3 + m
                t_o = mm(PSt[:, 2 + par, m * 128:m * 128 + 128], dl[:, h_, :], pa[:, h_, :], False, True,
                         m == 2 and par == 1)
        dl_r[0] = dl_r[1] = [t_o]
        st["d"] = [t_dl]
        for n in ("Kd", "Vb", "QgT", "WT", "PAT"):
            r2[n].free[o[n]] = [t_o]
        a = act(ho(OT), PSt[:, 2:4, 0:384], ACT.Copy, t_o, st["ot"])
        a2 = act(ho(O2), PSt[:, 2:4, 0:384], ACT.Square, st["o2"])
        st["o"] = [a2]
        for par in range(2):
            w = slice(64 * par, 64 * par + 64)
            o2 = O2[w, 3 * par:3 * par + 3, :]
            o["t_o2"] = tt(V, o2, o2, Q2[o["Q2"]][w, :, :], ALU.add, a2, o["t_q2"])
        r2["Q2"].free[o["Q2"]] = [o["t_o2"]]
        gr, t_g_ = gl[u]
        o["t_og"] = tt(G, OT[:, :, :], OT[:, :, :], UG[gr][:, :, :], ALU.mult, a, t_g_)
        g_ring.free[gr] = [o["t_og"]]
        if u + 2 < 16:
            load_g(u + 2)
        yield

    x1_slots, x1_ring = slots(2), Ring(2)
    t_x1 = {}

    def post(u):
        s, b = u // 4, u % 4
        r = got[u]
        p, free = pairs.take()
        PE.wait(free, r["t_o2"])
        for par in range(2):
            t = mm(PSt[:, 4 + 2 * p + par, 0:384], C["ON"], O2[:, 3 * par:3 * par + 3, :], True, True, par == 1)
        st["o2"] = [t]
        a = act(ho(R), PSt[:, 4 + 2 * p:6 + 2 * p, 0:384], ACT.Ln, t, st["r"])
        pfree(p, a)
        a = act(R[:, :, :], R[:, :, :], ACT.Exp, a, scale=-0.5)
        yield
        a = tt(V, OZ[:, :, :], OT[:, :, :], R[:, :, :], ALU.mult, a, r["t_og"], st["oz"])
        st["ot"] = [a]
        st["r"] = [a]
        hi = act(OZh[:, :, :], OZ[:, :, :], ACT.Copy, a, st["ozs"])
        yield
        lo = tt(V, OZl[:, :, :], OZ[:, :, :], OZh[:, :, :].bitcast(f32), ALU.subtract, hi, st["ozs"])
        st["oz"] = [lo]
        yield
        p, free = pairs.take()
        PE.wait(free, lo, o["t_wo"])
        for h_ in range(6):
            t = mm3(bank(4 + 2 * p), OZh[:, h_, :], OZl[:, h_, :], Woh[:, h_, :], Wol[:, h_, :], h_ == 0, h_ == 5,
                    h_ == 5)
        st["ozs"] = [t]
        xr, t_x = xbl[u]
        k, free = x1_ring.take()
        a = tt(V, YB[k][:, :], bank(4 + 2 * p), gaB[:, b, :], ALU.mult, t, o["t_ga"], free)
        pfree(p, a)
        a = tt(G, YB[k][:, :], YB[k][:, :], XB[xr][:, :], ALU.add, a, t_x)
        xb_ring.free[xr] = [a]
        yield
        t_r = rstd(u, YB[k][:, :], [a])
        t_x1[u] = x1_slots[k].start(SY, scrX[u], YB[k][:, :], a)
        x1_ring.free[k] = [t_x1[u], t_r]
        if u + 2 < 16:
            load_xb(u + 2)
        yield

    graw_slot = slots(1)[0]
    graw_free = []
    gw = Ring(4)

    def split_ff(r, t):
        nonlocal graw_free
        a = act(Ghi[r][:, :, :], Graw[:, :, :], ACT.Copy, t, gw.free[r])
        b_ = tt(V, Glo[r][:, :, :], Graw[:, :, :], Ghi[r][:, :, :].bitcast(f32), ALU.subtract, a, gw.free[r])
        graw_free = [b_]
        return b_

    def load_ff(j):
        t = graw_slot.start(SY, Graw[:, :, :], wg[j], graw_free)
        r, free = gw.take()
        return r, split_ff(r, t)

    fw = {}

    def weave(*gens):
        gens = [g_ for g_ in gens if g_ is not None]
        while gens:
            for g_ in list(gens):
                if next(g_, "end") == "end":
                    gens.remove(g_)

    t_hc, t_gb = {}, None
    f_norm = Ring(2)
    HF0 = [at(top + 8192 + i * 2048, [128, 4, 128]) for i in range(2)]

    def first_norms():
        nonlocal t_gb
        f_norm.free = [[st["o"]], [st["o"]]]
        for n, _ in enumerate(norms(order[0:4], lambda n: (XF[n], xf[n], None), False, [None, None], HF0, 2, 3,
                                    [t_sb, t_cb, last_rec], f_norm, 2, t_hc, V)):
            if n == 6:
                SC.wait(last_rec)
                t_gb = gate_rows(1, gbB)
            yield

    sb = setup_b()
    next(sb)
    weave(prep(0))
    f_gen = None
    for u in range(17):
        weave(rec(u) if u < 16 else None, prep(u + 1) if u < 15 else None, post(u - 1) if u else None,
              f_gen if u == 16 else sb if u == 0 else None, f_gen if u == 16 else None)
        if u == 8:
            p_read = (PE.sem, PE.n)
            t_graw = graw_slot.start(SY, Graw[:, :, :], wg[0], p_read)
        if u == 13:
            p_read = (PE.sem, PE.n)
            xf_slots = slots(6)
            xf = [xf_slots[n].start(SY, XF[n], scrX[order[n]], t_x1[order[n]], p_read) for n in range(6)]
        if u == 14:
            for n in range(6):
                v = order[n]
                xf[n] = ts(V, XF[n], XF[n], mv[:, v, 0:1], rs[:, v:v + 1], ALU.subtract, ALU.mult, xf[n],
                           (SC.sem, SC.n))
        if u == 15:
            last_rec = [(E_.sem, E_.n) for E_ in (PE, V, SC, G)]
            f_gen = first_norms()
            for _ in range(3):
                next(f_gen)
        if u == 10:
            fw[0] = (gw.take()[0], split_ff(0, t_graw))
            fw[1] = (gw.take()[0], graw_slot.start(SY, Graw[:, :, :], wg[1], graw_free))

    allB = [(E_.sem, E_.n) for E_ in (PE, V, SC, G)] + [xb_ring.free, u_ring.free, g_ring.free]
    gw.free[3] = [x1_ring.free]
    for E_ in (V, SC, G, SY):
        E_.wait(allB)
    SC.q.append(lambda e: e.preload_act_table_set("silu_and_others"))
    hf_free[:] = [[], []]
    xn_free[:] = [[], []]
    n_ring = Ring(2)
    n_ring.free = [pairs.free[1], pairs.free[1]]
    pairs.free = [pairs.free[0] + pairs.free[1]] * 2
    xc_slots, xc_ring = slots(4), Ring(4)

    def load_xc(u, *w):
        r, free = xc_ring.take()
        return r, xc_slots[r].start(SY, XC[r][:, :], scrX[u], t_x1[u], free, *w)

    xl = {}

    def src_c(n):
        if n < 2:
            return XF[n + 4], xf[n + 4], None
        rd = []
        r, t = xl[n + 4]
        xc_ring.free[r] = rd
        return XC[r][:, :], t, rd

    def norm_c():
        xc_ring.n = 2
        xl[6], xl[7] = load_xc(order[6]), load_xc(order[7])
        for n, _ in enumerate(norms(order[4:], src_c, False, XNC, HFC, 2, 3, [t_sb, t_cb], n_ring, 6, t_hc)):
            if n >= 3 and n + 5 < 16:
                xl[n + 5] = load_xc(order[n + 5])
            yield

    nrm = norm_c()
    next(nrm)
    next(nrm)
    fw[1] = (1, split_ff(1, fw[1][1]))
    gub = Ring(4)
    gub.free = [[st["d"]], [st["d"]], f_norm.free[0], f_norm.free[1]]
    yb = Ring(2)
    yb.free = [[pairs.free[0]], [pairs.free[1]]]
    si_ring, f_ring = Ring(2), Ring(4)
    gf_free = []
    t_y = {}
    outs = []
    xo = {}
    NG = 8

    def gate_up(q, b, step):
        nonlocal gf_free
        fs = []
        for jj in range(2):
            w, tw = fw[2 * q + jj]
            i1, free1 = gub.take()
            i2, free2 = gub.take()
            PE.wait(free1, free2, tw, t_hc[12 + b])
            for n, i in ((0, i1), (1, i2)):
                for k in range(4):
                    kk = slice(k * 128, (k + 1) * 128)
                    t = mm3(bank(i), Ghi[w][:, n, kk], Glo[w][:, n, kk], Hhi[:, b, k, :], Hlo[:, b, k, :], k == 0,
                            k == 3, k == 3)
                if n == 0:
                    z, free = si_ring.take()
                    t_si = act(SI[z][:, :], bank(i), ACT.Silu, t, free)
                    gub.free[i] = [t_si]
                    step()
            a = tt(V, GF[:, :], bank(i2), SI[z][:, :], ALU.mult, t, t_si, gf_free)
            gub.free[i2] = [a]
            si_ring.free[z] = [a]
            k, free = f_ring.take()
            hi = act(FH[k][:, :], GF[:, :], ACT.Copy, a, free)
            lo = tt(V, FL[k][:, :], GF[:, :], FH[k][:, :].bitcast(f32), ALU.subtract, hi, free)
            gf_free = [lo]
            fs.append((k, w, lo))
            step()
        return fs

    def down(q, b, fs, step):
        for s in range(4):
            u = s * 4 + b
            i, free = yb.take()
            PE.wait(free, fs[0][2], fs[1][2])
            for n, (k, w, _) in enumerate(fs):
                tk = slice(s * 128, (s + 1) * 128)
                t = mm3(bank(4 + i), FH[k][:, tk], FL[k][:, tk], Ghi[w][:, 2, :], Glo[w][:, 2, :], n == 0, n == 1,
                        n == 1)
            if q == 0:
                t_y[u] = cp(V, ya(u), bank(4 + i), t, t_hc[5])
            else:
                t_y[u] = tt(V, ya(u), bank(4 + i), ya(u), ALU.add, t, t_y[u])
            yb.free[i] = [t_y[u]]
            if q == NG - 1:
                r, t_x = xo[u]
                a = tt(V, ya(u), ya(u), gbB[:, b, :], ALU.mult, t_y[u], t_gb)
                a = tt(V if u == 15 else G, ya(u), ya(u), XC[r][:, :], ALU.add, a, t_x)
                xc_ring.free[r] = [a]
                outs.append(Slot(sem()).start(SY, out[b, s * 128:(s + 1) * 128, :], ya(u), a))
            step()
        for k, w, _ in fs:
            f_ring.free[k] = [t]
        if b == 3:
            for k, w, _ in fs:
                gw.free[w] = [t]

    def steps(n):
        return lambda: [next(nrm, None) for _ in range(n)]

    pend = None
    for q in range(NG):
        for b in range(4):
            if q == 0 and b:
                while 12 + b not in t_hc:
                    next(nrm)
            fs = gate_up(q, b, steps(0 if q else 1 if b else 2))
            if pend is not None:
                down(*pend, steps(0))
            pend = (q, b, fs)
            if q == NG - 1:
                for s in range(4):
                    xo[s * 4 + b] = load_xc(s * 4 + b)
            if b == 1 and q + 1 < NG:
                for j in (2 * q + 2, 2 * q + 3):
                    fw[j] = load_ff(j)
            if q == 0 and b == 3:
                for _ in nrm:
                    pass
                yb.n, yb.i = 4, 1
                yb.free += [[t_hc[15]], [t_hc[15]]]
                xc_ring.n, xc_ring.free = 4, xc_ring.free[0:2] + [[t_hc[15]], [t_hc[15]]]
    down(*pend, steps(0))
    SY.wait(outs)

    with nc.Block() as block:
        @block.sync
        def _(e):
            SY.run(e)

        @block.tensor
        def _(e):
            PE.run(e)

        @block.vector
        def _(e):
            V.run(e)

        @block.scalar
        def _(e):
            SC.run(e)

        @block.gpsimd
        def _(e):
            G.run(e)


def tiles(w, n):
    return np.ascontiguousarray(w.reshape(4, 128, n, 128).transpose(2, 1, 0, 3))


def kernel(**inputs):
    import concourse.bacc as bacc
    from concourse.bass_utils import run_bass_kernel_spmd

    v = {k: np.asarray(a) for k, a in inputs.items()}
    A = lambda n: v["L0_attn_" + n]
    wab = np.zeros((D, 128), np.float32)
    wab[:, 0:6] = A("Wa")[:, HEADS]
    wab[:, 6:12] = A("Wb")[:, HEADS]
    hv = lambda w: w.reshape(D, H, DV)[:, HEADS].reshape(D, H * DV)
    W1 = np.concatenate([tiles(wab, 1), tiles(A("Wk"), 3), tiles(A("Wq"), 3), tiles(hv(A("Wv")), 6),
                         tiles(hv(A("Wg")), 6)])
    cw = np.concatenate([A("conv_wk").reshape(3, 128, 4), A("conv_wq").reshape(3, 128, 4),
                         A("conv_wv").reshape(H, DV, 4)[HEADS]]).transpose(1, 0, 2)
    row = lambda a: np.broadcast_to(a[None, :], (128, H))
    gate, up = tiles(v["L0_ffn_w_gate"].T, 16), tiles(v["L0_ffn_w_up"].T, 16)
    down = v["L0_ffn_w_down"].T.reshape(16, 128, 1, D)
    arrays = {
        "x": v["L0_attn_hidden_states"],
        "W1": W1,
        "cw": cw,
        "dtb": row(A("dt_bias")[HEADS]),
        "alog": row(A("A_log")[HEADS]),
        "nw": A("norm_weight").reshape(128, 1),
        "Wo": A("Wo").reshape(H, DV, D)[HEADS].transpose(1, 0, 2),
        "cT": v["L0_c"].T.reshape(4, 128, 4).transpose(1, 0, 2),
        "wmod": v["L0_wmod"].reshape(4, 128, 6 * D).transpose(1, 0, 2),
        "wf": np.concatenate([gate.reshape(16, 128, 1, D), up.reshape(16, 128, 1, D), down], axis=2),
        "cst": constants(),
    }
    arrays = {k: np.ascontiguousarray(a) for k, a in arrays.items()}
    nc = bacc.Bacc("TRN2", target_bir_lowering=False, num_devices=1)
    h = {k: nc.dram_tensor("in_" + k, a.shape, mybir.dt.from_np(a.dtype), kind="ExternalInput").ap()
         for k, a in arrays.items()}
    out = nc.dram_tensor("out", (NB, SEQ, D), mybir.dt.float32, kind="ExternalOutput").ap()
    build(nc, h["x"], h["W1"], h["cw"], h["dtb"], h["alog"], h["nw"], h["Wo"], h["cT"], h["wmod"], h["wf"], h["cst"],
          out)
    r = run_bass_kernel_spmd(nc, [{"in_" + k: a for k, a in arrays.items()}], core_ids=[0])
    return r.results[0]["out"]
```
